# Optimizing a Trainium2 kernel written in Bass

```python
import numpy as np
import jax
import jax.numpy as jnp

def _softmax(x, axis=-1):
    return jax.nn.softmax(x, axis=axis)

def _gelu(x):
    return jax.nn.gelu(x, approximate=True)

def _silu(x):
    return jax.nn.silu(x)

def _sigmoid(x):
    return jax.nn.sigmoid(x)

def _layernorm(x, axis=-1, eps=1e-05):
    m = jnp.mean(x, axis=axis, keepdims=True)
    v = jnp.var(x, axis=axis, keepdims=True)
    return (x - m) / jnp.sqrt(v + eps)

def _scatter_add(tgt, idx, src, axis=0):
    return tgt.at[idx].add(src)

def _segment_sum(src, seg, n):
    return jax.ops.segment_sum(src, seg, n)
kernel_name = 'mk_gnn_preln_d1_gnn_r64_32add0'

def setup_inputs(seed: int=0):
    np.random.seed(seed)
    _w = jnp.asarray

    def _rec_inputs():
        import jax
        import jax.numpy as jnp
        _gk = jax.random.key(seed)
        x = -0.0005121 + 1.001 * jax.random.normal(jax.random.fold_in(_gk, 1), (100000, 64), jnp.float32)
        src = jax.random.randint(jax.random.fold_in(_gk, 2), (25000,), 0, 100000, jnp.int32)
        dst = jnp.minimum((100000 * jax.random.uniform(jax.random.fold_in(_gk, 3), (25000,)) ** 2.0).astype(jnp.int32), 99999)
        _o = jnp.argsort(dst, stable=True)
        src = src[_o]
        dst = dst[_o]
        edge_attr_64 = -9.77346e-05 + 0.999888 * jax.random.normal(jax.random.fold_in(_gk, 11), (25000, 64), jnp.float32)
        return (x, src, dst, edge_attr_64)
    x, src, dst, edge_attr_64 = _rec_inputs()

    def _L0_gnn_setup():
        import jax, jax.numpy as jnp
        import numpy as np
        N_NODES = 50000
        N_EDGES = 12500
        D_NODE = 64
        D_EDGE = 64
        HIDDEN = 128
        key = jax.random.key(seed)
        k1, k2, k3, k4, k5 = jax.random.split(key, 5)
        x_node = jax.random.normal(k1, (N_NODES, D_NODE), dtype=jnp.float32)
        x_edge = jax.random.normal(k2, (N_EDGES, D_EDGE), dtype=jnp.float32)
        edge_index = jax.random.randint(k3, (2, N_EDGES), 0, N_NODES, dtype=jnp.int64)
        d_in = D_NODE + D_EDGE
        W1 = jax.random.normal(k4, (d_in, HIDDEN), dtype=jnp.float32) / np.sqrt(d_in)
        b1 = jnp.zeros((HIDDEN,), dtype=jnp.float32)
        W2 = jax.random.normal(k5, (HIDDEN, D_NODE), dtype=jnp.float32) / np.sqrt(HIDDEN)
        b2 = jnp.zeros((D_NODE,), dtype=jnp.float32)
        return {'x_node': x_node, 'x_edge': x_edge, 'edge_index': edge_index, 'W1': W1, 'b1': b1, 'W2': W2, 'b2': b2}
    _L0_gnn_all = _L0_gnn_setup()
    _L0_gnn_in = {k: v for k, v in _L0_gnn_all.items() if k in ('W1', 'b1', 'W2', 'b2')}
    del _L0_gnn_all
    return {'x': x, 'src': src, 'dst': dst, 'edge_attr_64': edge_attr_64, 'L0_gnn_W1': _L0_gnn_in['W1'], 'L0_gnn_b1': _L0_gnn_in['b1'], 'L0_gnn_W2': _L0_gnn_in['W2'], 'L0_gnn_b2': _L0_gnn_in['b2']}

def reference(x, src, dst, edge_attr_64, L0_gnn_W1, L0_gnn_b1, L0_gnn_W2, L0_gnn_b2):
    import jax
    import jax.numpy as jnp

    def _L0_gnn_ref(x_node, x_edge, edge_index, W1, b1, W2, b2):
        import jax, jax.numpy as jnp
        import numpy as np
        N_NODES = 50000
        N_EDGES = 12500
        D_NODE = 64
        D_EDGE = 64
        HIDDEN = 128
        agg = jnp.zeros((x_node.shape[0], x_edge.shape[1]), dtype=x_edge.dtype)
        agg = agg.at[edge_index[0]].add(x_edge)
        agg = agg.at[edge_index[1]].add(x_edge)
        h = jnp.concatenate([x_node, agg], axis=1)
        h = jax.nn.relu(h @ W1 + b1)
        x_node_ = h @ W2 + b2
        return x_node_
    edge_index = jnp.stack([src, dst])
    h = jnp.maximum(_layernorm(x, axis=-1), 0.0)
    x = x + _L0_gnn_ref(h, edge_attr_64, edge_index, L0_gnn_W1, L0_gnn_b1, L0_gnn_W2, L0_gnn_b2)
    return x

_drawn_inputs = setup_inputs


def setup_inputs(seed=0):
    import zlib

    import numpy as np

    out = dict(_drawn_inputs(seed))
    spreads = {'L0_gnn_b1': (0.0, 0.1), 'L0_gnn_b2': (0.0, 0.1)}
    factors = {}
    for name, (base, spread) in spreads.items():
        noise = np.random.default_rng([zlib.crc32(name.encode()), seed]).standard_normal(out[name].shape)
        drawn = base * np.exp(spread * noise) if base else spread * noise
        out[name] = jnp.asarray(drawn.astype(out[name].dtype))
    for name, factor in factors.items():
        out[name] = (out[name] * factor).astype(out[name].dtype)
    return out
```

```python
import concourse.bass as bass
from concourse import mybir
from contextlib import ExitStack

f32 = mybir.dt.float32
bf16 = mybir.dt.bfloat16
i32 = mybir.dt.int32
ALU = mybir.AluOpType
ACT = mybir.ActivationFunctionType
AX = mybir.AxisListType

P = 128
N_NODES, D = 100000, 64
N_EDGES = 25000
HID = 128
EPS = 1e-5

EC = 7
BATCH = P * EC
N_BATCH = -(-N_EDGES // BATCH)
LAST_EDGE = N_EDGES - BATCH
SEEN = BATCH * (N_BATCH - 1) - LAST_EDGE
N_ADDS = 2 * N_BATCH
PARK = N_NODES
SPARE = N_NODES + 1
AGG_ROWS = N_NODES + 1024
ZERO_PARTS = 8
ZERO_COLS = AGG_ROWS * D // P // ZERO_PARTS

R = 16
TILE = P * R
N_TILES = -(-N_NODES // TILE)
LAST_NODE = N_NODES - TILE
GR = 4
GROUPS = R // GR
N_GROUPS = N_TILES * GROUPS
SLOTS = 4


def gnn_program(nc, x, src, dst, edge_attr, w1, b1, w2, b2, out):
    assert N_BATCH % 2 == 0 and (N_TILES - 1) % SLOTS == 0 and AGG_ROWS * D == P * ZERO_PARTS * ZERO_COLS
    agg = nc.dram_tensor("agg", (AGG_ROWS, D), f32, kind="Internal").ap()

    with ExitStack() as ctx:
        def sb(name, shape, dt):
            return ctx.enter_context(nc.sbuf_tensor(name, shape, dt))

        def sem(name):
            return ctx.enter_context(nc.semaphore(name))

        zeros = sb("zeros", [P, ZERO_COLS], f32)
        ident = sb("ident", [P, P], f32)
        earlier = sb("earlier", [P, BATCH], f32)
        spare_i = sb("spare_i", [P, EC], i32)
        spare = sb("spare", [P, EC], f32)
        w1_sb = sb("w1_sb", [P, HID], f32)
        w2_sb = sb("w2_sb", [HID, D], f32)
        b1_sb = sb("b1_sb", [HID, 1], f32)
        b2_row = sb("b2_row", [1, D], f32)
        b2_rest = sb("b2_rest", [1, 2, D], f32)
        b2_parts = sb("b2_parts", [1, 3, GR, D], bf16)
        ones_row = sb("ones_row", [1, P], bf16)
        nodes_i = sb("nodes_i", [P, 2, N_BATCH, EC], i32)
        nodes_f = sb("nodes_f", [P, 2, N_BATCH, EC], f32)
        cur = sb("cur", [P, 2, EC], f32)
        edges = sb("edges", [P, 2, EC, D], f32)
        rest = sb("rest", [P, EC, D], f32)
        parts = sb("parts", [P, 2, 3, EC, D], bf16)
        same = sb("same", [P, 2, EC, BATCH], bf16)
        count = sb("count", [P, 2, EC], f32)
        offset = sb("offset", [P, 2, EC], f32)
        target = sb("target", [P, 2, EC], i32)
        sums = sb("sums", [P, 2, EC, D], f32)
        xt = sb("xt", [P, SLOTS, R, D], f32)
        xc = sb("xc", [P, SLOTS, R, D], f32)
        sq = sb("sq", [P, 2, R, D], f32)
        ha = sb("ha", [P, SLOTS, R, 2, D], f32)
        yt = sb("yt", [P, SLOTS, R, D], f32)
        stat = sb("stat", [P, 2, 8, R], f32)
        feat_T = sb("feat_T", [P, 2, GR * P], f32)
        hid_T = sb("hid_T", [HID, 2, GR * P], f32)

        banks = ctx.enter_context(nc.psum_tensor("banks", [P, 8, 512], f32))

        s_filled = sem("s_filled")
        s_const = sem("s_const")
        s_ones = sem("s_ones")
        s_b2_parts = sem("s_b2_parts")
        s_zero_src = sem("s_zero_src")
        s_zeroed = sem("s_zeroed")
        s_ids = sem("s_ids")
        s_ids_f = sem("s_ids_f")
        s_spare = sem("s_spare")
        s_masked = sem("s_masked")
        s_w = sem("s_w")
        s_b2 = sem("s_b2")
        s_edges = [sem(f"s_edges{n}") for n in range(2)]
        s_hi = sem("s_hi")
        s_rest = sem("s_rest")
        s_mid = sem("s_mid")
        s_rest2 = sem("s_rest2")
        s_parts = sem("s_parts")
        s_cur = sem("s_cur")
        s_row = sem("s_row")
        s_same = sem("s_same")
        s_off = sem("s_off")
        s_target = sem("s_target")
        s_summed = sem("s_summed")
        s_sums = sem("s_sums")
        s_added = sem("s_added")
        s_adding = sem("s_adding")
        s_x = [sem(f"s_x{n}") for n in range(SLOTS)]
        s_agg = [sem(f"s_agg{n}") for n in range(SLOTS)]
        s_stored = [sem(f"s_stored{n}") for n in range(SLOTS)]
        s_total = sem("s_total")
        s_mean = sem("s_mean")
        s_xc = sem("s_xc")
        s_sq = sem("s_sq")
        s_relu = sem("s_relu")
        s_var = sem("s_var")
        s_std = sem("s_std")
        s_newton = sem("s_newton")
        s_rstd = sem("s_rstd")
        s_h = sem("s_h")
        s_tr = sem("s_tr")
        s_featd = sem("s_featd")
        s_feata = sem("s_feata")
        s_mm1 = sem("s_mm1")
        s_hid = sem("s_hid")
        s_mm2 = sem("s_mm2")
        s_y = sem("s_y")

        block = ctx.enter_context(nc.Block())

        def row_bank(l):
            return banks[:, 2 * l:2 * l + 2, :].rearrange("p b n -> p (b n)")[:, 0:BATCH]

        def sum_bank(l):
            return banks[:, 4 + l, 0:EC * D]

        def edge_steps(eng, body, tail=1):
            body(0)
            with eng.Fori(1, N_BATCH // 2 - tail) as i:
                body(i)
            for i in range(N_BATCH // 2 - tail, N_BATCH // 2):
                body(i)

        def is_last_pair(i):
            return isinstance(i, int) and i == N_BATCH // 2 - 1

        def tile_steps(eng, body):
            for tt in range(SLOTS):
                body(0, tt)
            with eng.Fori(1, (N_TILES - 1) // SLOTS - 1) as i:
                for tt in range(SLOTS):
                    body(i, tt)
            for tt in range(SLOTS + 1):
                body((N_TILES - 1) // SLOTS - 1, tt)

        def exists(i, tt):
            return not isinstance(i, int) or SLOTS * i + tt < N_TILES

        @block.sync
        def _(sp):
            ids = [src, dst]
            for l in range(2):
                full = BATCH * (N_BATCH - 1)
                sp.dma_start(nodes_i[:, l, 0:N_BATCH - 1, :],
                             ids[l][0:full].rearrange("(b p c) -> p b c", p=P, c=EC)).then_inc(s_ids, 16)
                sp.dma_start(nodes_i[:, l, N_BATCH - 1, :],
                             ids[l][LAST_EDGE:N_EDGES].rearrange("(p c) -> p c", c=EC)).then_inc(s_ids, 16)

            def load_edges(i, h, b):
                first = LAST_EDGE if isinstance(i, int) and b == N_BATCH - 1 else b * BATCH
                sp.dma_start(edges[:, h, :, :],
                             edge_attr[bass.ds(first, BATCH), :].rearrange("(p c) f -> p c f", c=EC))\
                    .then_inc(s_edges[h], 16)

            load_edges(0, 0, 0)
            load_edges(0, 1, 1)
            sp.wait_ge(s_zero_src, 1)
            agg_flat = agg.rearrange("a f -> (a f)")
            for k in range(ZERO_PARTS):
                n = P * ZERO_COLS
                sp.dma_start(agg_flat[k * n:(k + 1) * n].rearrange("(p f) -> p f", p=P), zeros[:, :])\
                    .then_inc(s_zeroed, 16)
            sp.dma_start(w1_sb[:, :], w1[:, :]).then_inc(s_w, 16)
            sp.dma_start(w2_sb[:, :], w2[:, :]).then_inc(s_w, 16)
            sp.dma_start(b1_sb[:, :], b1.rearrange("(p a) -> p a", a=1)).then_inc(s_w, 16)
            sp.dma_start(b2_row[:, :], b2.rearrange("(a n) -> a n", a=1)).then_inc(s_b2, 16)

            def steps(i):
                if is_last_pair(i):
                    return
                for h in range(2):
                    sp.wait_ge(s_parts, 2 * i + (h + 1))
                    load_edges(i, h, 2 * i + (2 + h))
            edge_steps(sp, steps, tail=2)

            def load_x(i, tt):
                first = LAST_NODE if isinstance(i, int) and SLOTS * i + tt == N_TILES - 1 else (SLOTS * i + tt) * TILE
                s = tt % SLOTS
                sp.dma_start(xt[:, s, :, :], x[bass.ds(first, TILE), :].rearrange("(p r) f -> p r f", r=R))\
                    .then_inc(s_x[s], 16)

            def load_agg(i, tt):
                first = LAST_NODE if isinstance(i, int) and SLOTS * i + tt == N_TILES - 1 else (SLOTS * i + tt) * TILE
                s = tt % SLOTS
                sp.dma_start(ha[:, s, :, 1, :], agg[bass.ds(first, TILE), :].rearrange("(p r) f -> p r f", r=R))\
                    .then_inc(s_agg[s], 16)

            for tt in range(SLOTS):
                load_x(0, tt)
            sp.wait_ge(s_added, 16 * EC * N_ADDS)
            for tt in range(SLOTS):
                load_agg(0, tt)

            def tile(i, tt):
                s = tt % SLOTS
                t = SLOTS * i + tt
                first = LAST_NODE if isinstance(t, int) and t == N_TILES - 1 else t * TILE
                sp.wait_ge(s_y, GROUPS * t + GROUPS)
                if isinstance(t, int) and t == N_TILES - 1:
                    sp.wait_ge(s_stored[(s + SLOTS - 1) % SLOTS], 16 * (N_TILES // SLOTS))
                sp.dma_start(out[bass.ds(first, TILE), :].rearrange("(p r) f -> p r f", r=R), yt[:, s, :, :])\
                    .then_inc(s_stored[s], 16)
                if exists(i, tt + SLOTS):
                    load_x(i + 1, tt)
                    load_agg(i + 1, tt)
            tile_steps(sp, tile)
            for s in range(SLOTS):
                sp.wait_ge(s_stored[s], 16 * len(range(s, N_TILES, SLOTS)))

        @block.gpsimd
        def _(pool):
            pool.memset(ident[:, :], 0.0).then_inc(s_filled, 1)
            pool.memset(earlier[:, :], 1.0).then_inc(s_filled, 1)
            pool.wait_ge(s_filled, 2)
            pool.affine_select(out=ident[:, :], in_=ident[:, :], compare_op=ALU.not_equal, fill=1.0,
                               base=0, pattern=[[-1, P]], channel_multiplier=1).then_inc(s_const, 1)
            pool.affine_select(out=earlier[:, :], in_=earlier[:, :], compare_op=ALU.is_ge, fill=0.0,
                               base=BATCH - P, pattern=[[-1, BATCH]], channel_multiplier=1).then_inc(s_const, 1)
            pool.iota(spare_i[:, :], pattern=[[P, EC]], base=SPARE, channel_multiplier=1).then_inc(s_spare, 1)
            pool.wait_ge(s_ids_f, 1)
            last = nodes_f[:, :, N_BATCH - 1, :]
            pool.affine_select(out=last, in_=last, compare_op=ALU.is_ge, fill=float(PARK), base=-SEEN,
                               pattern=[[0, 2], [1, EC]], channel_multiplier=EC).then_inc(s_masked, 1)

            def steps(i):
                for h in range(2):
                    for l in range(2):
                        n = 4 * i + (2 * h + l)
                        pool.wait_ge(s_target, n + 1)
                        pool.wait_ge(s_sums, n + 1)
                        if not (isinstance(n, int) and n == 0):
                            pool.wait_ge(s_added, 16 * EC * n)
                        pool.wait_ge(s_zeroed, 16 * ZERO_PARTS)
                        pool.sem_inc(s_adding, 1)
                        for c in range(EC):
                            pool.indirect_dma_start(
                                agg[:, :], bass.IndirectOffsetOnAxis(ap=target[:, l, c:c + 1], axis=0),
                                sums[:, l, c, :], None, compute_op=ALU.add)\
                                .then_inc(s_added, 16)
            edge_steps(pool, steps)

            def center(i, tt):
                t = SLOTS * i + tt
                s = tt % SLOTS
                pool.wait_ge(s_mean, t + 1)
                mean = stat[:, tt % 2, 1, :].unsqueeze(2).to_broadcast([P, R, D])
                pool.tensor_tensor(out=xc[:, s, :, :], in0=xt[:, s, :, :], in1=mean, op=ALU.add).then_inc(s_xc, 1)

            def scale(i, tt):
                t = SLOTS * i + tt
                s = tt % SLOTS
                pool.wait_ge(s_relu, t + 1)
                pool.wait_ge(s_rstd, t + 1)
                if not (isinstance(t, int) and t < SLOTS):
                    pool.wait_ge(s_tr, GROUPS * t - GROUPS * (SLOTS - 1))
                rstd = stat[:, tt % 2, 7, :].unsqueeze(2).to_broadcast([P, R, D])
                pool.tensor_tensor(out=ha[:, s, :, 0, :], in0=xc[:, s, :, :], in1=rstd, op=ALU.mult).then_inc(s_h, 1)

            center(0, 0)
            center(0, 1)
            scale(0, 0)
            scale(0, 1)

            def tile(i, tt):
                if exists(i, tt + 2):
                    center(i, tt + 2)
                    scale(i, tt + 2)
            tile_steps(pool, tile)

        @block.vector
        def _(dve):
            nc.vector.memset(zeros[:, :], 0.0).then_inc(s_zero_src, 1)
            nc.vector.memset(ones_row[:, :], 1.0).then_inc(s_ones, 1)
            dve.wait_ge(s_ids, 64)
            nc.vector.tensor_copy(nodes_f[:, :, :, :], nodes_i[:, :, :, :]).then_inc(s_ids_f, 1)
            dve.wait_ge(s_spare, 1)
            nc.vector.tensor_copy(spare[:, :], spare_i[:, :]).then_inc(s_spare, 1)

            def split(b, h):
                dve.wait_ge(s_hi, b + 1)
                nc.vector.tensor_tensor(out=rest[:, :, :], in0=edges[:, h, :, :], in1=parts[:, h, 0, :, :],
                                        op=ALU.subtract).then_inc(s_rest, 1)
                dve.wait_ge(s_mid, b + 1)
                nc.vector.tensor_tensor(out=parts[:, h, 2, :, :], in0=rest[:, :, :], in1=parts[:, h, 1, :, :],
                                        op=ALU.subtract).then_inc(s_parts, 1)

            split(0, 0)
            for k in range(3):
                row = b2_row[:, :] if k == 0 else b2_rest[:, k - 1, :]
                if k == 0:
                    dve.wait_ge(s_b2, 16)
                else:
                    dve.wait_ge(s_b2_parts, 2 * k)
                nc.vector.tensor_copy(b2_parts[:, k, :, :], row.unsqueeze(1).to_broadcast([1, GR, D]))\
                    .then_inc(s_b2_parts, 1)
                if k < 2:
                    dve.wait_ge(s_b2_parts, 2 * k + 1)
                    nc.vector.tensor_tensor(out=b2_rest[:, k, :], in0=row, in1=b2_parts[:, k, 0, :],
                                            op=ALU.subtract).then_inc(s_b2_parts, 1)
            dve.wait_ge(s_const, 2)
            dve.wait_ge(s_spare, 2)

            def steps(i):
                for h in range(2):
                    for l in range(2):
                        n = 4 * i + (2 * h + l)
                        dve.wait_ge(s_row, n + 1)
                        if not (isinstance(n, int) and n < 2):
                            dve.wait_ge(s_summed, n - 1)
                        for c in range(EC):
                            w = P * (c + 1)
                            last = nc.vector.scalar_tensor_tensor(
                                out=same[:, l, c, 0:w], in0=row_bank(l)[:, 0:w], scalar=cur[:, l, c:c + 1],
                                in1=earlier[:, BATCH - w:BATCH], op0=ALU.is_equal, op1=ALU.mult,
                                accum_out=count[:, l, c:c + 1])
                            last.then_inc(s_same, 1)
                        nc.vector.tensor_tensor(out=offset[:, l, :], in0=cur[:, l, :], in1=spare[:, :],
                                                op=ALU.subtract).then_inc(s_off, 1)
                        dve.wait_ge(s_off, 2 * n + 1)
                        dve.wait_ge(s_same, EC * n + EC)
                        nc.vector.scalar_tensor_tensor(out=offset[:, l, :], in0=count[:, l, :], scalar=1.0,
                                                       in1=offset[:, l, :], op0=ALU.is_equal, op1=ALU.mult)\
                            .then_inc(s_off, 1)
                        dve.wait_ge(s_off, 2 * n + 2)
                        if not (isinstance(n, int) and n < 2):
                            dve.wait_ge(s_added, 16 * EC * n - 16 * EC)
                        nc.vector.tensor_tensor(out=target[:, l, :], in0=offset[:, l, :], in1=spare[:, :],
                                                op=ALU.add).then_inc(s_target, 1)
                        if l == 0 and not (is_last_pair(i) and h == 1):
                            split(2 * i + (h + 1), 1 - h)
            edge_steps(dve, steps)

            def stats_a(i, tt):
                t = SLOTS * i + tt
                s = tt % SLOTS
                st = stat[:, tt % 2, :, :]
                dve.wait_ge(s_x[s], 16 * i + 16 * (1 + tt // SLOTS))
                nc.vector.tensor_reduce(out=st[:, 0, :], in_=xt[:, s, :, :], axis=AX.X, op=ALU.add).then_inc(s_total, 1)
                dve.wait_ge(s_total, t + 1)
                if not (isinstance(t, int) and t < 2):
                    dve.wait_ge(s_xc, t - 1)
                nc.vector.tensor_scalar(st[:, 1, :], st[:, 0, :], -1.0 / D, None, ALU.mult).then_inc(s_mean, 1)

            def stats_b(i, tt):
                t = SLOTS * i + tt
                st = stat[:, tt % 2, :, :]
                dve.wait_ge(s_sq, t + 1)
                nc.vector.tensor_reduce(out=st[:, 2, :], in_=sq[:, tt % 2, :, :], axis=AX.X, op=ALU.add)\
                    .then_inc(s_newton, 1)
                dve.wait_ge(s_newton, 5 * t + 1)
                nc.vector.tensor_scalar(st[:, 3, :], st[:, 2, :], 1.0 / D, EPS, ALU.mult, ALU.add).then_inc(s_var, 1)
                dve.wait_ge(s_std, t + 1)
                nc.vector.reciprocal(st[:, 5, :], st[:, 4, :]).then_inc(s_newton, 1)
                dve.wait_ge(s_newton, 5 * t + 2)
                nc.vector.tensor_tensor(out=st[:, 6, :], in0=st[:, 5, :], in1=st[:, 5, :], op=ALU.mult)\
                    .then_inc(s_newton, 1)
                dve.wait_ge(s_newton, 5 * t + 3)
                nc.vector.tensor_tensor(out=st[:, 6, :], in0=st[:, 6, :], in1=st[:, 3, :], op=ALU.mult)\
                    .then_inc(s_newton, 1)
                dve.wait_ge(s_newton, 5 * t + 4)
                nc.vector.tensor_scalar(st[:, 6, :], st[:, 6, :], -0.5, 1.5, ALU.mult, ALU.add).then_inc(s_newton, 1)
                dve.wait_ge(s_newton, 5 * t + 5)
                if not (isinstance(t, int) and t < 2):
                    dve.wait_ge(s_h, t - 1)
                nc.vector.tensor_tensor(out=st[:, 7, :], in0=st[:, 6, :], in1=st[:, 5, :], op=ALU.mult)\
                    .then_inc(s_rstd, 1)

            def feat(t, g):
                k = GROUPS * t + g
                if g % 2:
                    return
                dve.wait_ge(s_tr, k + 1)
                if not (isinstance(k, int) and k < 2):
                    dve.wait_ge(s_mm1, k - 1)
                nc.vector.tensor_copy(feat_T[:, g % 2, :], banks[:, g % 2, :]).then_inc(s_featd, 1)

            def finish(i, tt, g):
                t = SLOTS * i + tt
                s = tt % SLOTS
                k = GROUPS * t + g
                dve.wait_ge(s_mm2, k + 1)
                if g == 0 and not (isinstance(t, int) and t < SLOTS):
                    dve.wait_ge(s_stored[s], 16 * i + 16 * (tt // SLOTS))
                rows = slice(GR * g, GR * g + GR)
                nc.vector.tensor_tensor(out=yt[:, s, rows, :],
                                        in0=banks[:, 4 + g % 2, 0:GR * D].rearrange("p (r f) -> p r f", f=D),
                                        in1=xt[:, s, rows, :], op=ALU.add).then_inc(s_y, 1)

            stats_a(0, 0)
            stats_a(0, 1)
            stats_b(0, 0)
            stats_b(0, 1)
            feat(0, 0)
            feat(0, 1)

            def tile(i, tt):
                t = SLOTS * i + tt
                for g in range(GROUPS):
                    if g == 0 and exists(i, tt + 2):
                        stats_a(i, tt + 2)
                    if g == 2 and exists(i, tt + 2):
                        stats_b(i, tt + 2)
                    if g < 2:
                        feat(t, g + 2)
                    elif exists(i, tt + 1):
                        feat(t + 1, g - 2)
                    finish(i, tt, g)
            tile_steps(dve, tile)

        @block.scalar
        def _(act):
            def current(n, l, b):
                if not (isinstance(n, int) and n < 2):
                    act.wait_ge(s_target, n - 1)
                nc.scalar.copy(cur[:, l, :], nodes_f[:, l, b, :] if isinstance(b, int)
                               else nodes_f[:, l, bass.ds(b, 1), :].rearrange("p a c -> p (a c)")).then_inc(s_cur, 1)

            def split(i, b, h, off):
                act.wait_ge(s_edges[h], 16 * i + 16 * off)
                if not (isinstance(b, int) and b < 2):
                    act.wait_ge(s_summed, 2 * b - 2)
                nc.scalar.copy(parts[:, h, 0, :, :], edges[:, h, :, :]).then_inc(s_hi, 1)
                act.wait_ge(s_rest, b + 1)
                nc.scalar.copy(parts[:, h, 1, :, :], rest[:, :, :]).then_inc(s_mid, 1)

            act.wait_ge(s_masked, 1)
            split(0, 0, 0, 1)
            current(0, 0, 0)
            current(1, 1, 0)

            def steps(i):
                for h in range(2):
                    for l in range(2):
                        n = 4 * i + (2 * h + l)
                        if not (is_last_pair(i) and h == 1):
                            current(n + 2, l, 2 * i + (h + 1))
                        if l == 0 and not (is_last_pair(i) and h == 1):
                            split(i, 2 * i + (h + 1), 1 - h, 1 + h)
                        act.wait_ge(s_summed, n + 1)
                        if not (isinstance(n, int) and n < 2):
                            act.wait_ge(s_added, 16 * EC * n - 16 * EC)
                        nc.scalar.copy(sums[:, l, :, :].rearrange("p c f -> p (c f)"), sum_bank(l)).then_inc(s_sums, 1)
            edge_steps(act, steps)

            def stats(i, tt):
                t = SLOTS * i + tt
                s = tt % SLOTS
                act.wait_ge(s_xc, t + 1)
                if not (isinstance(t, int) and t < 2):
                    act.wait_ge(s_newton, 5 * t - 9)
                nc.scalar.activation(sq[:, tt % 2, :, :], xc[:, s, :, :], ACT.Square).then_inc(s_sq, 1)
                act.wait_ge(s_sq, t + 1)
                nc.scalar.activation(xc[:, s, :, :], xc[:, s, :, :], ACT.Relu).then_inc(s_relu, 1)
                act.wait_ge(s_var, t + 1)
                nc.scalar.activation(stat[:, tt % 2, 4, :], stat[:, tt % 2, 3, :], ACT.Sqrt).then_inc(s_std, 1)

            def feat(t, g):
                k = GROUPS * t + g
                if g % 2 == 0:
                    return
                act.wait_ge(s_tr, k + 1)
                if not (isinstance(k, int) and k < 2):
                    act.wait_ge(s_mm1, k - 1)
                nc.scalar.copy(feat_T[:, g % 2, :], banks[:, g % 2, :]).then_inc(s_feata, 1)

            def hidden(t, g):
                k = GROUPS * t + g
                act.wait_ge(s_mm1, k + 1)
                if not (isinstance(k, int) and k < 2):
                    act.wait_ge(s_mm2, k - 1)
                nc.scalar.activation(hid_T[:, g % 2, :], banks[:, 2 + g % 2, :], ACT.Relu, bias=b1_sb[:, 0:1])\
                    .then_inc(s_hid, 1)

            stats(0, 0)
            stats(0, 1)
            act.wait_ge(s_w, 48)
            feat(0, 1)
            hidden(0, 0)

            def tile(i, tt):
                t = SLOTS * i + tt
                for g in range(GROUPS):
                    if g == 1 and exists(i, tt + 2):
                        stats(i, tt + 2)
                    if g < 2:
                        feat(t, g + 2)
                    elif exists(i, tt + 1):
                        feat(t + 1, g - 2)
                    if g < GROUPS - 1:
                        hidden(t, g + 1)
                    elif exists(i, tt + 1):
                        hidden(t + 1, 0)
            tile_steps(act, tile)

        @block.tensor
        def _(pe):
            def rows(n, l):
                pe.wait_ge(s_cur, n + 1)
                if not (isinstance(n, int) and n < 2):
                    pe.wait_ge(s_same, EC * n - EC)
                for c in range(EC):
                    last = nc.tensor.transpose(row_bank(l)[:, P * c:P * (c + 1)],
                                               cur[:, l, c:c + 1].to_broadcast([P, P]), ident[:, :])
                last.then_inc(s_row, 1)

            pe.wait_ge(s_const, 2)
            rows(0, 0)

            def steps(i):
                for h in range(2):
                    for l in range(2):
                        n = 4 * i + (2 * h + l)
                        if not (isinstance(n, int) and n == N_ADDS - 1):
                            rows(n + 1, 1 - l)
                        pe.wait_ge(s_same, EC * n + EC)
                        pe.wait_ge(s_parts, 2 * i + (h + 1))
                        if not (isinstance(n, int) and n < 2):
                            pe.wait_ge(s_sums, n - 1)
                        for c in range(EC):
                            for c2 in range(c, EC):
                                for k in range(3):
                                    last = nc.tensor.matmul(sum_bank(l)[:, D * c:D * (c + 1)],
                                                            same[:, l, c2, P * c:P * (c + 1)],
                                                            parts[:, h, k, c2, :],
                                                            start=(c2 == c and k == 0), stop=(c2 == EC - 1 and k == 2))
                        last.then_inc(s_summed, 1)
            edge_steps(pe, steps)

            def transposes(i, tt, g):
                t = SLOTS * i + tt
                s = tt % SLOTS
                k = GROUPS * t + g
                if g == 0:
                    pe.wait_ge(s_h, t + 1)
                    pe.wait_ge(s_agg[s], 16 * i + 16 * (1 + tt // SLOTS))
                if not (isinstance(k, int) and k < 2):
                    if g % 2:
                        pe.wait_ge(s_feata, 2 * t + (g - 1) // 2)
                    else:
                        pe.wait_ge(s_featd, 2 * t + g // 2)
                for j in range(GR):
                    last = nc.tensor.transpose(banks[:, g % 2, P * j:P * (j + 1)],
                                               ha[:, s, GR * g + j, :, :].rearrange("p a f -> p (a f)"), ident[:, :])
                last.then_inc(s_tr, 1)

            def mm1(t, g):
                k = GROUPS * t + g
                if g % 2:
                    pe.wait_ge(s_feata, 2 * t + (g + 1) // 2)
                else:
                    pe.wait_ge(s_featd, 2 * t + g // 2 + 1)
                if not (isinstance(k, int) and k < 2):
                    pe.wait_ge(s_hid, k - 1)
                nc.tensor.matmul(banks[:, 2 + g % 2, :], w1_sb[:, :], feat_T[:, g % 2, :],
                                 start=True, stop=True).then_inc(s_mm1, 1)

            def mm2(t, g):
                k = GROUPS * t + g
                pe.wait_ge(s_hid, k + 1)
                if not (isinstance(k, int) and k < 2):
                    pe.wait_ge(s_y, k - 1)
                acc = banks[:, 4 + g % 2, 0:GR * D]
                for part in range(3):
                    nc.tensor.matmul(acc, ones_row[:, :], b2_parts[:, part, :, :].rearrange("a r f -> a (r f)"),
                                     start=(part == 0), stop=False)
                for j in range(GR):
                    last = nc.tensor.matmul(acc[:, D * j:D * (j + 1)], hid_T[:, g % 2, P * j:P * (j + 1)],
                                            w2_sb[:, :], start=False, stop=(j == GR - 1))
                last.then_inc(s_mm2, 1)

            pe.wait_ge(s_w, 48)
            pe.wait_ge(s_b2_parts, 5)
            pe.wait_ge(s_ones, 1)
            transposes(0, 0, 0)
            transposes(0, 0, 1)
            mm1(0, 0)

            def tile(i, tt):
                t = SLOTS * i + tt
                for g in range(GROUPS):
                    if g < 2:
                        transposes(i, tt, g + 2)
                    elif exists(i, tt + 1):
                        transposes(i, tt + 1, g - 2)
                    if g < GROUPS - 1:
                        mm1(t, g + 1)
                    elif exists(i, tt + 1):
                        mm1(t + 1, 0)
                    mm2(t, g)
            tile_steps(pe, tile)


_INS = ['x', 'src', 'dst', 'edge_attr_64', 'L0_gnn_W1', 'L0_gnn_b1', 'L0_gnn_W2', 'L0_gnn_b2']


def kernel(**inputs):
    import numpy as _np
    import concourse.bacc as _bacc
    from concourse import mybir as _mybir
    from concourse.bass_utils import run_bass_kernel_spmd as _run

    nc = _bacc.Bacc("TRN2", target_bir_lowering=False, num_devices=1)
    arrays, args = {}, []
    for name in _INS:
        a = _np.ascontiguousarray(inputs[name])
        arrays[f"in_{name}"] = a
        args.append(nc.dram_tensor(f"in_{name}", a.shape, _mybir.dt.from_np(a.dtype), kind="ExternalInput").ap())
    result = nc.dram_tensor("out", (N_NODES, D), _mybir.dt.float32, kind="ExternalOutput").ap()
    gnn_program(nc, *args, result)
    r = _run(nc, [arrays], core_ids=[0])
    return r.results[0]["out"]
```

```python
import concourse.bass as bass
from concourse import mybir
from contextlib import ExitStack

f32 = mybir.dt.float32
bf16 = mybir.dt.bfloat16
i32 = mybir.dt.int32
ALU = mybir.AluOpType
ACT = mybir.ActivationFunctionType
AX = mybir.AxisListType

P = 128
N_NODES, D = 100000, 64
N_EDGES = 25000
HID = 128
EPS = 1e-5

EC = 10
BATCH = P * EC
N_BATCH = -(-N_EDGES // BATCH)
LAST_EDGE = N_EDGES - BATCH
SEEN = BATCH * (N_BATCH - 1) - LAST_EDGE
N_ADDS = 2 * N_BATCH
PARK = N_NODES
SPARE = N_NODES + 1
AGG_ROWS = N_NODES + 1312
ZERO_PARTS = 16
ZERO_COLS = AGG_ROWS * D // P // ZERO_PARTS

R = 16
TILE = P * R
N_TILES = -(-N_NODES // TILE)
LAST_NODE = N_NODES - TILE
GR = 4
GROUPS = R // GR
N_GROUPS = N_TILES * GROUPS
SLOTS = 4
AHEAD = 4
assert SPARE + BATCH <= AGG_ROWS


def gnn_program(nc, x, src, dst, edge_attr, w1, b1, w2, b2, out):
    assert N_BATCH % 2 == 0 and (N_TILES - 1) % SLOTS == 0 and AGG_ROWS * D == P * ZERO_PARTS * ZERO_COLS
    agg = nc.dram_tensor("agg", (AGG_ROWS, D), f32, kind="Internal").ap()

    with ExitStack() as ctx:
        def sb(name, shape, dt):
            return ctx.enter_context(nc.sbuf_tensor(name, shape, dt))

        def sem(name):
            return ctx.enter_context(nc.semaphore(name))

        ident = sb("ident", [P, P], f32)
        earlier = sb("earlier", [P, BATCH], f32)
        spare_i = sb("spare_i", [P, EC], i32)
        spare = sb("spare", [P, EC], f32)
        w1_sb = sb("w1_sb", [P, HID], f32)
        w2_sb = sb("w2_sb", [HID, D], f32)
        b1_sb = sb("b1_sb", [HID, 1], f32)
        b2_all = sb("b2_all", [P, D], f32)
        nodes_i = sb("nodes_i", [P, 2, N_BATCH, EC], i32)
        nodes_f = sb("nodes_f", [P, 2, N_BATCH, EC], f32)
        cur = sb("cur", [P, 2, EC], f32)
        edges = sb("edges", [P, 2, EC, D], f32)
        rest = sb("rest", [P, EC, D], f32)
        parts = sb("parts", [P, 2, 3, EC, D], bf16)
        same = sb("same", [P, 2, EC, BATCH], bf16)
        count = sb("count", [P, 2, EC], f32)
        offset = sb("offset", [P, 2, EC], f32)
        target = sb("target", [P, 2, EC], i32)
        sums = sb("sums", [P, 2, EC, D], f32)
        xt = sb("xt", [P, SLOTS, R, D], f32)
        xb = sb("xb", [P, SLOTS, R, D], f32)
        xc = sb("xc", [P, SLOTS, R, D], f32)
        sq = sb("sq", [P, 2, R, D], f32)
        ha = sb("ha", [P, SLOTS, R, 2, D], f32)
        yt = sb("yt", [P, SLOTS, R, D], f32)
        stat = sb("stat", [P, SLOTS, 8, R], f32)
        zeros = yt.rearrange("p s r f -> p (s r f)")[:, 0:ZERO_COLS]
        feat_T = sb("feat_T", [P, 2, GR * P], f32)
        hid_T = sb("hid_T", [HID, 2, GR * P], f32)

        banks = ctx.enter_context(nc.psum_tensor("banks", [P, 8, 512], f32))

        s_filled = sem("s_filled")
        s_const = sem("s_const")
        s_zero_src = sem("s_zero_src")
        s_zeroed = sem("s_zeroed")
        s_ids = sem("s_ids")
        s_ids_f = sem("s_ids_f")
        s_spare = sem("s_spare")
        s_masked = sem("s_masked")
        s_w = sem("s_w")
        s_b2 = sem("s_b2")
        s_edges = [sem(f"s_edges{n}") for n in range(2)]
        s_hi = sem("s_hi")
        s_rest = sem("s_rest")
        s_mid = sem("s_mid")
        s_rest2 = sem("s_rest2")
        s_parts = sem("s_parts")
        s_cur = sem("s_cur")
        s_row = sem("s_row")
        s_same = sem("s_same")
        s_off = sem("s_off")
        s_target = sem("s_target")
        s_summed = sem("s_summed")
        s_sums = sem("s_sums")
        s_added = sem("s_added")
        s_adding = sem("s_adding")
        s_x = [sem(f"s_x{n}") for n in range(SLOTS)]
        s_agg = [sem(f"s_agg{n}") for n in range(SLOTS)]
        s_stored = [sem(f"s_stored{n}") for n in range(SLOTS)]
        s_total = sem("s_total")
        s_mean = sem("s_mean")
        s_xc = sem("s_xc")
        s_sq = sem("s_sq")
        s_relu = sem("s_relu")
        s_var = sem("s_var")
        s_std = sem("s_std")
        s_ssq = sem("s_ssq")
        s_newton = sem("s_newton")
        s_xb = sem("s_xb")
        s_rstd = sem("s_rstd")
        s_h = sem("s_h")
        s_tr = sem("s_tr")
        s_featd = sem("s_featd")
        s_feata = sem("s_feata")
        s_mm1 = sem("s_mm1")
        s_hid = sem("s_hid")
        s_mm2 = sem("s_mm2")
        s_y = sem("s_y")

        block = ctx.enter_context(nc.Block())

        row_bank = banks[:, 0:3, :].rearrange("p b n -> p (b n)")[:, 0:BATCH]

        def sum_bank(l):
            return banks[:, 3 + 2 * l:5 + 2 * l, :].rearrange("p b n -> p (b n)")[:, 0:EC * D]

        def at_least(eng, semaphore, value):
            if not isinstance(value, int) or value > 0:
                eng.wait_ge(semaphore, value)

        def edge_steps(eng, body, tail=1):
            body(0)
            with eng.Fori(1, N_BATCH // 2 - tail) as i:
                body(i)
            for i in range(N_BATCH // 2 - tail, N_BATCH // 2):
                body(i)

        def is_last_pair(i):
            return isinstance(i, int) and i == N_BATCH // 2 - 1

        def tile_steps(eng, body, tail=1):
            rounds = (N_TILES - 1) // SLOTS
            for tt in range(SLOTS):
                body(0, tt)
            with eng.Fori(1, rounds - tail) as i:
                for tt in range(SLOTS):
                    body(i, tt)
            for i in range(rounds - tail, rounds):
                for tt in range(SLOTS):
                    body(i, tt)
            body(rounds, 0)

        def exists(tile):
            return not isinstance(tile, int) or 0 <= tile < N_TILES

        def first_node(tile):
            return LAST_NODE if isinstance(tile, int) and tile == N_TILES - 1 else tile * TILE

        @block.sync
        def _(sp):
            ids = [src, dst]
            for l in range(2):
                full = BATCH * (N_BATCH - 1)
                sp.dma_start(nodes_i[:, l, 0:N_BATCH - 1, :],
                             ids[l][0:full].rearrange("(b p c) -> p b c", p=P, c=EC)).then_inc(s_ids, 16)
                sp.dma_start(nodes_i[:, l, N_BATCH - 1, :],
                             ids[l][LAST_EDGE:N_EDGES].rearrange("(p c) -> p c", c=EC)).then_inc(s_ids, 16)

            def load_edges(i, h, b):
                first = LAST_EDGE if isinstance(i, int) and b == N_BATCH - 1 else b * BATCH
                sp.dma_start(edges[:, h, :, :],
                             edge_attr[bass.ds(first, BATCH), :].rearrange("(p c) f -> p c f", c=EC))\
                    .then_inc(s_edges[h], 16)

            load_edges(0, 0, 0)
            load_edges(0, 1, 1)
            def load_x(i, tt):
                tile = SLOTS * i + tt
                if not exists(tile):
                    return
                at_least(sp, s_xb, tile - (SLOTS - 1))
                sp.dma_start(xt[:, tt % SLOTS, :, :],
                             x[bass.ds(first_node(tile), TILE), :].rearrange("(p r) f -> p r f", r=R))\
                    .then_inc(s_x[tt % SLOTS], 16)

            sp.dma_start(b2_all[:, :], b2.rearrange("(a n) -> a n", a=1).to_broadcast([P, D])).then_inc(s_b2, 16)
            for tt in range(SLOTS):
                load_x(0, tt)
            sp.wait_ge(s_zero_src, 1)
            agg_flat = agg.rearrange("a f -> (a f)")
            for k in range(ZERO_PARTS):
                n = P * ZERO_COLS
                sp.dma_start(agg_flat[k * n:(k + 1) * n].rearrange("(p f) -> p f", p=P), zeros)\
                    .then_inc(s_zeroed, 16)
            load_x(0, SLOTS)
            load_x(0, SLOTS + 1)
            sp.dma_start(w1_sb[:, :], w1[:, :]).then_inc(s_w, 16)
            sp.dma_start(w2_sb[:, :], w2[:, :]).then_inc(s_w, 16)
            sp.dma_start(b1_sb[:, :], b1.rearrange("(p a) -> p a", a=1)).then_inc(s_w, 16)

            def steps(i):
                if is_last_pair(i):
                    return
                for h in range(2):
                    sp.wait_ge(s_parts, 2 * i + (h + 1))
                    load_edges(i, h, 2 * i + (2 + h))
            edge_steps(sp, steps, tail=2)

            def load_agg(i, tt):
                tile = SLOTS * i + tt
                if not exists(tile):
                    return
                at_least(sp, s_tr, GROUPS * tile - GROUPS * (SLOTS - 1))
                sp.dma_start(ha[:, tt % SLOTS, :, 1, :],
                             agg[bass.ds(first_node(tile), TILE), :].rearrange("(p r) f -> p r f", r=R))\
                    .then_inc(s_agg[tt % SLOTS], 16)

            sp.wait_ge(s_added, 16 * EC * N_ADDS)
            for tt in range(SLOTS - 1):
                load_agg(0, tt)

            def step(i, tt):
                t = SLOTS * i + tt
                s = tt % SLOTS
                load_agg(i, tt + SLOTS - 1)
                load_x(i, tt + SLOTS + 2)
                sp.wait_ge(s_y, GROUPS * t + GROUPS)
                if isinstance(t, int) and t == N_TILES - 1:
                    sp.wait_ge(s_stored[(s + SLOTS - 1) % SLOTS], 16 * (N_TILES // SLOTS))
                sp.dma_start(out[bass.ds(first_node(t), TILE), :].rearrange("(p r) f -> p r f", r=R), yt[:, s, :, :])\
                    .then_inc(s_stored[s], 16)
            tile_steps(sp, step, tail=2)
            for s in range(SLOTS):
                sp.wait_ge(s_stored[s], 16 * len(range(s, N_TILES, SLOTS)))

        @block.gpsimd
        def _(pool):
            pool.memset(ident[:, :], 0.0).then_inc(s_filled, 1)
            pool.memset(earlier[:, :], 1.0).then_inc(s_filled, 1)
            pool.wait_ge(s_filled, 2)
            pool.affine_select(out=ident[:, :], in_=ident[:, :], compare_op=ALU.not_equal, fill=1.0,
                               base=0, pattern=[[-1, P]], channel_multiplier=1).then_inc(s_const, 1)
            pool.affine_select(out=earlier[:, :], in_=earlier[:, :], compare_op=ALU.is_ge, fill=0.0,
                               base=BATCH - P, pattern=[[-1, BATCH]], channel_multiplier=1).then_inc(s_const, 1)
            pool.iota(spare_i[:, :], pattern=[[P, EC]], base=SPARE, channel_multiplier=1).then_inc(s_spare, 1)
            pool.wait_ge(s_ids_f, 1)
            last = nodes_f[:, :, N_BATCH - 1, :]
            pool.affine_select(out=last, in_=last, compare_op=ALU.is_ge, fill=float(PARK), base=-SEEN,
                               pattern=[[0, 2], [1, EC]], channel_multiplier=EC).then_inc(s_masked, 1)

            def spread(a):
                return a.unsqueeze(2).to_broadcast([P, R, D])

            def with_b2(i, tt):
                tile = SLOTS * i + tt
                if not exists(tile):
                    return
                s = tt % SLOTS
                at_least(pool, s_y, GROUPS * tile - GROUPS * (SLOTS - 1))
                pool.tensor_tensor(out=xb[:, s, :, :], in0=xt[:, s, :, :],
                                   in1=b2_all[:, :].unsqueeze(1).to_broadcast([P, R, D]), op=ALU.add).then_inc(s_xb, 1)

            def scale(i, tt):
                tile = SLOTS * i + tt
                if not exists(tile):
                    return
                s = tt % SLOTS
                pool.wait_ge(s_relu, tile + 1)
                pool.wait_ge(s_rstd, tile + 1)
                at_least(pool, s_tr, GROUPS * tile - GROUPS * (SLOTS - 1))
                pool.tensor_tensor(out=ha[:, s, :, 0, :], in0=xc[:, s, :, :], in1=spread(stat[:, s, 7, :]),
                                   op=ALU.mult).then_inc(s_h, 1)

            def center(i, tt):
                tile = SLOTS * i + tt
                if not exists(tile):
                    return
                s = tt % SLOTS
                pool.wait_ge(s_mean, tile + 1)
                at_least(pool, s_h, tile - (SLOTS - 1))
                pool.tensor_tensor(out=xc[:, s, :, :], in0=xt[:, s, :, :], in1=spread(stat[:, s, 1, :]),
                                   op=ALU.add).then_inc(s_xc, 1)

            def step(i, tt):
                with_b2(i, tt + AHEAD - 1)
                scale(i, tt + AHEAD - 2)
                center(i, tt + AHEAD)

            pool.wait_ge(s_b2, 16)
            for tt in range(-AHEAD, 0):
                step(0, tt)

            def steps(i):
                for h in range(2):
                    for l in range(2):
                        n = 4 * i + (2 * h + l)
                        pool.wait_ge(s_target, n + 1)
                        pool.wait_ge(s_sums, n + 1)
                        if not (isinstance(n, int) and n == 0):
                            pool.wait_ge(s_added, 16 * EC * n)
                        pool.wait_ge(s_zeroed, 16 * ZERO_PARTS)
                        pool.sem_inc(s_adding, 1)
                        for c in range(EC):
                            pool.indirect_dma_start(
                                agg[:, :], bass.IndirectOffsetOnAxis(ap=target[:, l, c:c + 1], axis=0),
                                sums[:, l, c, :], None, compute_op=ALU.add)\
                                .then_inc(s_added, 16)
            edge_steps(pool, steps)

            tile_steps(pool, step)

        @block.vector
        def _(dve):
            nc.vector.memset(zeros, 0.0).then_inc(s_zero_src, 1)
            dve.wait_ge(s_ids, 64)
            nc.vector.tensor_copy(nodes_f[:, :, :, :], nodes_i[:, :, :, :]).then_inc(s_ids_f, 1)
            dve.wait_ge(s_spare, 1)
            nc.vector.tensor_copy(spare[:, :], spare_i[:, :]).then_inc(s_spare, 1)

            def split(b, h):
                dve.wait_ge(s_hi, b + 1)
                nc.vector.tensor_tensor(out=rest[:, :, :], in0=edges[:, h, :, :], in1=parts[:, h, 0, :, :],
                                        op=ALU.subtract).then_inc(s_rest, 1)
                dve.wait_ge(s_mid, b + 1)
                nc.vector.tensor_tensor(out=parts[:, h, 2, :, :], in0=rest[:, :, :], in1=parts[:, h, 1, :, :],
                                        op=ALU.subtract).then_inc(s_parts, 1)

            def totals(i, tt):
                tile = SLOTS * i + tt
                if not exists(tile):
                    return
                s = tt % SLOTS
                dve.wait_ge(s_x[s], 16 * i + 16 * (1 + tt // SLOTS))
                nc.vector.tensor_reduce(out=stat[:, s, 0, :], in_=xt[:, s, :, :], axis=AX.X, op=ALU.add)\
                    .then_inc(s_total, 1)
                dve.wait_ge(s_total, tile + 1)
                at_least(dve, s_xc, tile - (SLOTS - 1))
                nc.vector.tensor_scalar(stat[:, s, 1, :], stat[:, s, 0, :], -1.0 / D, None, ALU.mult)\
                    .then_inc(s_mean, 1)

            def variance(i, tt):
                tile = SLOTS * i + tt
                if not exists(tile):
                    return
                s = tt % SLOTS
                dve.wait_ge(s_sq, tile + 1)
                nc.vector.tensor_reduce(out=stat[:, s, 2, :], in_=sq[:, tt % 2, :, :], axis=AX.X, op=ALU.add)\
                    .then_inc(s_ssq, 1)
                dve.wait_ge(s_ssq, tile + 1)
                nc.vector.tensor_scalar(stat[:, s, 3, :], stat[:, s, 2, :], 1.0 / D, EPS, ALU.mult, ALU.add)\
                    .then_inc(s_var, 1)

            def inverse(i, tt):
                tile = SLOTS * i + tt
                if not exists(tile):
                    return
                st = stat[:, tt % SLOTS, :, :]
                dve.wait_ge(s_std, tile + 1)
                nc.vector.reciprocal(st[:, 5, :], st[:, 4, :]).then_inc(s_newton, 1)
                dve.wait_ge(s_newton, 4 * tile + 1)
                nc.vector.tensor_tensor(out=st[:, 6, :], in0=st[:, 5, :], in1=st[:, 5, :], op=ALU.mult)\
                    .then_inc(s_newton, 1)
                dve.wait_ge(s_newton, 4 * tile + 2)
                nc.vector.tensor_tensor(out=st[:, 6, :], in0=st[:, 6, :], in1=st[:, 3, :], op=ALU.mult)\
                    .then_inc(s_newton, 1)
                dve.wait_ge(s_newton, 4 * tile + 3)
                nc.vector.tensor_scalar(st[:, 6, :], st[:, 6, :], -0.5, 1.5, ALU.mult, ALU.add).then_inc(s_newton, 1)
                dve.wait_ge(s_newton, 4 * tile + 4)
                at_least(dve, s_h, tile - (SLOTS - 1))
                nc.vector.tensor_tensor(out=st[:, 7, :], in0=st[:, 6, :], in1=st[:, 5, :], op=ALU.mult)\
                    .then_inc(s_rstd, 1)

            for tt in range(-AHEAD, 0):
                inverse(0, tt + AHEAD - 2)
                totals(0, tt + AHEAD)
                variance(0, tt + AHEAD - 1)
            split(0, 0)
            dve.wait_ge(s_const, 2)
            dve.wait_ge(s_spare, 2)

            def steps(i):
                for h in range(2):
                    for l in range(2):
                        n = 4 * i + (2 * h + l)
                        dve.wait_ge(s_row, n + 1)
                        if not (isinstance(n, int) and n < 2):
                            dve.wait_ge(s_summed, n - 1)
                        for c in range(EC):
                            w = P * (c + 1)
                            last = nc.vector.scalar_tensor_tensor(
                                out=same[:, l, c, 0:w], in0=row_bank[:, 0:w], scalar=cur[:, l, c:c + 1],
                                in1=earlier[:, BATCH - w:BATCH], op0=ALU.is_equal, op1=ALU.mult,
                                accum_out=count[:, l, c:c + 1])
                            last.then_inc(s_same, 1)
                        nc.vector.tensor_tensor(out=offset[:, l, :], in0=cur[:, l, :], in1=spare[:, :],
                                                op=ALU.subtract).then_inc(s_off, 1)
                        dve.wait_ge(s_off, 2 * n + 1)
                        dve.wait_ge(s_same, EC * n + EC)
                        nc.vector.scalar_tensor_tensor(out=offset[:, l, :], in0=count[:, l, :], scalar=1.0,
                                                       in1=offset[:, l, :], op0=ALU.is_equal, op1=ALU.mult)\
                            .then_inc(s_off, 1)
                        dve.wait_ge(s_off, 2 * n + 2)
                        if not (isinstance(n, int) and n < 2):
                            dve.wait_ge(s_added, 16 * EC * n - 16 * EC)
                        nc.vector.tensor_tensor(out=target[:, l, :], in0=offset[:, l, :], in1=spare[:, :],
                                                op=ALU.add).then_inc(s_target, 1)
                        if l == 0 and not (is_last_pair(i) and h == 1):
                            split(2 * i + (h + 1), 1 - h)
            edge_steps(dve, steps)

            def feat(t, g):
                k = GROUPS * t + g
                if g % 2:
                    return
                dve.wait_ge(s_tr, k + 1)
                if not (isinstance(k, int) and k < 2):
                    dve.wait_ge(s_mm1, k - 1)
                nc.vector.tensor_copy(feat_T[:, g % 2, :], banks[:, g % 2, :]).then_inc(s_featd, 1)

            def finish(i, tt, g):
                t = SLOTS * i + tt
                s = tt % SLOTS
                k = GROUPS * t + g
                dve.wait_ge(s_mm2, k + 1)
                if g == 0:
                    at_least(dve, s_stored[s], 16 * i + 16 * (tt // SLOTS))
                rows = slice(GR * g, GR * g + GR)
                nc.vector.tensor_tensor(out=yt[:, s, rows, :],
                                        in0=banks[:, 4 + g % 2, 0:GR * D].rearrange("p (r f) -> p r f", f=D),
                                        in1=xb[:, s, rows, :], op=ALU.add).then_inc(s_y, 1)

            feat(0, 0)
            feat(0, 1)

            def step(i, tt):
                t = SLOTS * i + tt
                for g in range(GROUPS):
                    if g < 2:
                        feat(t, g + 2)
                    elif exists(t + 1):
                        feat(t + 1, g - 2)
                    if g == 1:
                        inverse(i, tt + AHEAD - 2)
                        totals(i, tt + AHEAD)
                    if g == 3:
                        variance(i, tt + AHEAD - 1)
                    finish(i, tt, g)
            tile_steps(dve, step)

        @block.scalar
        def _(act):
            def current(n, l, b):
                if not (isinstance(n, int) and n < 2):
                    act.wait_ge(s_target, n - 1)
                nc.scalar.copy(cur[:, l, :], nodes_f[:, l, b, :] if isinstance(b, int)
                               else nodes_f[:, l, bass.ds(b, 1), :].rearrange("p a c -> p (a c)")).then_inc(s_cur, 1)

            def split(i, b, h, off):
                act.wait_ge(s_edges[h], 16 * i + 16 * off)
                if not (isinstance(b, int) and b < 2):
                    act.wait_ge(s_summed, 2 * b - 2)
                nc.scalar.copy(parts[:, h, 0, :, :], edges[:, h, :, :]).then_inc(s_hi, 1)
                act.wait_ge(s_rest, b + 1)
                nc.scalar.copy(parts[:, h, 1, :, :], rest[:, :, :]).then_inc(s_mid, 1)

            def square(i, tt):
                tile = SLOTS * i + tt
                if not exists(tile):
                    return
                act.wait_ge(s_xc, tile + 1)
                at_least(act, s_ssq, tile - 1)
                nc.scalar.activation(sq[:, tt % 2, :, :], xc[:, tt % SLOTS, :, :], ACT.Square).then_inc(s_sq, 1)

            def relu(i, tt):
                tile = SLOTS * i + tt
                if not exists(tile):
                    return
                s = tt % SLOTS
                act.wait_ge(s_sq, tile + 1)
                nc.scalar.activation(xc[:, s, :, :], xc[:, s, :, :], ACT.Relu).then_inc(s_relu, 1)

            def root(i, tt):
                tile = SLOTS * i + tt
                if not exists(tile):
                    return
                s = tt % SLOTS
                act.wait_ge(s_var, tile + 1)
                nc.scalar.activation(stat[:, s, 4, :], stat[:, s, 3, :], ACT.Sqrt).then_inc(s_std, 1)

            for tt in range(-AHEAD, 0):
                relu(0, tt + AHEAD - 1)
                root(0, tt + AHEAD - 2)
                square(0, tt + AHEAD)
            act.wait_ge(s_masked, 1)
            split(0, 0, 0, 1)
            current(0, 0, 0)
            current(1, 1, 0)

            def steps(i):
                for h in range(2):
                    for l in range(2):
                        n = 4 * i + (2 * h + l)
                        if not (is_last_pair(i) and h == 1):
                            current(n + 2, l, 2 * i + (h + 1))
                        if l == 0 and not (is_last_pair(i) and h == 1):
                            split(i, 2 * i + (h + 1), 1 - h, 1 + h)
                        act.wait_ge(s_summed, n + 1)
                        if not (isinstance(n, int) and n < 2):
                            act.wait_ge(s_added, 16 * EC * n - 16 * EC)
                        nc.scalar.copy(sums[:, l, :, :].rearrange("p c f -> p (c f)"), sum_bank(l)).then_inc(s_sums, 1)
            edge_steps(act, steps)

            def feat(t, g):
                k = GROUPS * t + g
                if g % 2 == 0:
                    return
                act.wait_ge(s_tr, k + 1)
                if not (isinstance(k, int) and k < 2):
                    act.wait_ge(s_mm1, k - 1)
                nc.scalar.copy(feat_T[:, g % 2, :], banks[:, g % 2, :]).then_inc(s_feata, 1)

            def hidden(t, g):
                k = GROUPS * t + g
                act.wait_ge(s_mm1, k + 1)
                if not (isinstance(k, int) and k < 2):
                    act.wait_ge(s_mm2, k - 1)
                nc.scalar.activation(hid_T[:, g % 2, :], banks[:, 2 + g % 2, :], ACT.Relu, bias=b1_sb[:, 0:1])\
                    .then_inc(s_hid, 1)

            act.wait_ge(s_w, 48)
            feat(0, 1)
            hidden(0, 0)

            def step(i, tt):
                t = SLOTS * i + tt
                for g in range(GROUPS):
                    if g < 2:
                        feat(t, g + 2)
                    elif exists(t + 1):
                        feat(t + 1, g - 2)
                    if g == 0:
                        relu(i, tt + AHEAD - 1)
                        root(i, tt + AHEAD - 2)
                    if g == 3:
                        square(i, tt + AHEAD)
                    if g < GROUPS - 1:
                        hidden(t, g + 1)
                    elif exists(t + 1):
                        hidden(t + 1, 0)
            tile_steps(act, step)

        @block.tensor
        def _(pe):
            def rows(n, l):
                pe.wait_ge(s_cur, n + 1)
                at_least(pe, s_same, EC * n)
                for c in range(EC):
                    last = nc.tensor.transpose(row_bank[:, P * c:P * (c + 1)],
                                               cur[:, l, c:c + 1].to_broadcast([P, P]), ident[:, :])
                last.then_inc(s_row, 1)

            pe.wait_ge(s_const, 2)
            rows(0, 0)

            def steps(i):
                for h in range(2):
                    for l in range(2):
                        n = 4 * i + (2 * h + l)
                        pe.wait_ge(s_same, EC * n + EC)
                        if not (isinstance(n, int) and n == N_ADDS - 1):
                            rows(n + 1, 1 - l)
                        pe.wait_ge(s_parts, 2 * i + (h + 1))
                        if not (isinstance(n, int) and n < 2):
                            pe.wait_ge(s_sums, n - 1)
                        for c in range(EC):
                            for c2 in range(c, EC):
                                for k in range(3):
                                    last = nc.tensor.matmul(sum_bank(l)[:, D * c:D * (c + 1)],
                                                            same[:, l, c2, P * c:P * (c + 1)],
                                                            parts[:, h, k, c2, :],
                                                            start=(c2 == c and k == 0), stop=(c2 == EC - 1 and k == 2))
                        last.then_inc(s_summed, 1)
            edge_steps(pe, steps)

            def transposes(i, tt, g):
                t = SLOTS * i + tt
                s = tt % SLOTS
                k = GROUPS * t + g
                if g == 0:
                    pe.wait_ge(s_h, t + 1)
                    pe.wait_ge(s_agg[s], 16 * i + 16 * (1 + tt // SLOTS))
                if not (isinstance(k, int) and k < 2):
                    if g % 2:
                        pe.wait_ge(s_feata, 2 * t + (g - 1) // 2)
                    else:
                        pe.wait_ge(s_featd, 2 * t + g // 2)
                for j in range(GR):
                    last = nc.tensor.transpose(banks[:, g % 2, P * j:P * (j + 1)],
                                               ha[:, s, GR * g + j, :, :].rearrange("p a f -> p (a f)"), ident[:, :])
                last.then_inc(s_tr, 1)

            def mm1(t, g):
                k = GROUPS * t + g
                if g % 2:
                    pe.wait_ge(s_feata, 2 * t + (g + 1) // 2)
                else:
                    pe.wait_ge(s_featd, 2 * t + g // 2 + 1)
                at_least(pe, s_hid, k - 1)
                nc.tensor.matmul(banks[:, 2 + g % 2, :], w1_sb[:, :], feat_T[:, g % 2, :],
                                 start=True, stop=True).then_inc(s_mm1, 1)

            def mm2(t, g):
                k = GROUPS * t + g
                pe.wait_ge(s_hid, k + 1)
                at_least(pe, s_y, k - 1)
                acc = banks[:, 4 + g % 2, 0:GR * D]
                for j in range(GR):
                    last = nc.tensor.matmul(acc[:, D * j:D * (j + 1)], hid_T[:, g % 2, P * j:P * (j + 1)],
                                            w2_sb[:, :], start=True, stop=True)
                last.then_inc(s_mm2, 1)

            pe.wait_ge(s_w, 48)
            transposes(0, 0, 0)
            transposes(0, 0, 1)
            mm1(0, 0)

            def step(i, tt):
                t = SLOTS * i + tt
                for g in range(GROUPS):
                    if g < 2:
                        transposes(i, tt, g + 2)
                    elif exists(t + 1):
                        transposes(i, tt + 1, g - 2)
                    if g < GROUPS - 1:
                        mm1(t, g + 1)
                    elif exists(t + 1):
                        mm1(t + 1, 0)
                    mm2(t, g)
            tile_steps(pe, step)


_INS = ['x', 'src', 'dst', 'edge_attr_64', 'L0_gnn_W1', 'L0_gnn_b1', 'L0_gnn_W2', 'L0_gnn_b2']


def kernel(**inputs):
    import numpy as _np
    import concourse.bacc as _bacc
    from concourse import mybir as _mybir
    from concourse.bass_utils import run_bass_kernel_spmd as _run

    nc = _bacc.Bacc("TRN2", target_bir_lowering=False, num_devices=1)
    arrays, args = {}, []
    for name in _INS:
        a = _np.ascontiguousarray(inputs[name])
        arrays[f"in_{name}"] = a
        args.append(nc.dram_tensor(f"in_{name}", a.shape, _mybir.dt.from_np(a.dtype), kind="ExternalInput").ap())
    result = nc.dram_tensor("out", (N_NODES, D), _mybir.dt.float32, kind="ExternalOutput").ap()
    gnn_program(nc, *args, result)
    r = _run(nc, [arrays], core_ids=[0])
    return r.results[0]["out"]
```

```python
import concourse.bass as bass
from concourse import mybir
from contextlib import ExitStack

f32 = mybir.dt.float32
bf16 = mybir.dt.bfloat16
i32 = mybir.dt.int32
ALU = mybir.AluOpType
ACT = mybir.ActivationFunctionType
AX = mybir.AxisListType

P = 128
N_NODES, D = 100000, 64
N_EDGES = 25000
HID = 128
EPS = 1e-5

EC = 8
BATCH = P * EC
N_BATCH = -(-N_EDGES // BATCH)
NEW = N_EDGES - BATCH * (N_BATCH - 1)
LAST_EC = -(-NEW // P)
PARK = N_NODES
SPARE = N_NODES + 1
AGG_ROWS = N_NODES + 1056
ZERO_PARTS = 32
ZERO_COLS = AGG_ROWS * D // P // ZERO_PARTS
ZERO_FIRST, ZERO_STEP = 3, 6
EARLY = 4
RING = 6
ACT_FROM = 6

R = 16
TILE = P * R
N_TILES = -(-N_NODES // TILE)
GR = 4
GROUPS = R // GR
N_GROUPS = N_TILES * GROUPS
SLOTS = 4
AHEAD = 4
assert EARLY < RING and EC == 2 * LAST_EC
assert ZERO_FIRST + ZERO_STEP * RING >= ZERO_PARTS
assert SPARE + BATCH <= AGG_ROWS and N_BATCH % RING == 1 and RING > 3



def dst_adds_before(q):
    return EARLY - 1 + q // 2


def bound(j):
    return N_NODES - TILE * (2 * (j - EARLY) + 4)


def fills_before(j):
    return 6 + 2 * j


def low_bound(j):
    return AGG_ROWS - fills_before(j) * (AGG_ROWS // ZERO_PARTS)


def gnn_program(nc, x, src, dst, edge_attr, w1, b1, w2, b2, out):
    assert (N_TILES - 1) % SLOTS == 0 and AGG_ROWS * D == P * ZERO_PARTS * ZERO_COLS
    agg = nc.dram_tensor("agg", (AGG_ROWS, D), f32, kind="Internal").ap()

    with ExitStack() as ctx:
        def sb(name, shape, dt):
            return ctx.enter_context(nc.sbuf_tensor(name, shape, dt))

        def sem(name):
            return ctx.enter_context(nc.semaphore(name))

        ident = sb("ident", [P, P], f32)
        earlier = sb("earlier", [P, BATCH], f32)
        spare_i = sb("spare_i", [P, EC], i32)
        spare = sb("spare", [P, EC], f32)
        w1_sb = sb("w1_sb", [P, HID], f32)
        w2_sb = sb("w2_sb", [HID, D], f32)
        b1_sb = sb("b1_sb", [HID, 1], f32)
        b2_all = sb("b2_all", [P, D], f32)
        nodes_i = sb("nodes_i", [P, 2, N_BATCH, EC], i32)
        nodes_f = sb("nodes_f", [P, 2, N_BATCH, EC], f32)
        cur = sb("cur", [P, 2, EC], f32)
        edges = sb("edges", [P, 2, EC, D], f32)
        rest = sb("rest", [P, EC, D], f32)
        parts = sb("parts", [P, 2, 3, EC, D], bf16)
        count = sb("count", [P, 2, EC], f32)
        count_before = sb("count_before", [P, 2, EC - ACT_FROM], f32)
        offset = sb("offset", [P, EC], f32)
        src_offset = sb("src_offset", [P, 2, EC], f32)
        kept_offset = sb("kept_offset", [P, N_BATCH, EC], f32)
        kept_sums = sb("kept_sums", [P, N_BATCH, EC, D], f32)
        target = sb("target", [P, RING, EC], i32)
        sums = sb("sums", [P, RING, EC, D], f32)
        early_space = kept_sums.rearrange("p b c f -> p (b c f)")[:, 0:3 * N_BATCH * EC]\
            .rearrange("p (a b c) -> p a b c", a=3, c=EC)
        bounds_i = early_space[:, 0, :, :].bitcast(i32)
        bounds = early_space[:, 1, :, :]
        broken = early_space[:, 2, :, :]
        broken_sum = sb("broken_sum", [P, 1], f32)
        ones = sb("ones", [P, P], f32)
        rising = sb("rising", [P, 1], f32)
        falls = sb("falls", [P, 1], i32)
        xt = sb("xt", [P, SLOTS, R, D], f32)
        xb = sb("xb", [P, SLOTS, R, D], f32)
        xc = sb("xc", [P, SLOTS, R, D], f32)
        sq = sb("sq", [P, 2, R, D], f32)
        ha = sb("ha", [P, SLOTS, R, 2, D], f32)
        yt = sb("yt", [P, SLOTS, R, D], f32)
        same = ha.rearrange("p s r a f -> p (s r a f)").bitcast(bf16)\
            .rearrange("p (l c n) -> p l c n", l=2, n=BATCH)
        stat = sb("stat", [P, SLOTS, 8, R], f32)
        zeros = yt.rearrange("p s r f -> p (s r f)")[:, 0:ZERO_COLS]
        feat_T = sb("feat_T", [P, 2, GR * P], f32)
        hid_T = sb("hid_T", [HID, 2, GR * P], f32)
        distance = [t.rearrange("p a n -> p (a n)")[:, 0:BATCH - P] for t in (feat_T, hid_T)]

        banks = ctx.enter_context(nc.psum_tensor("banks", [P, 8, 512], f32))

        s_filled = sem("s_filled")
        s_const = sem("s_const")
        s_ones = sem("s_ones")
        s_zero_src = sem("s_zero_src")
        s_zeroed = [sem(f"s_zeroed{n}") for n in range(2)]
        s_ids = sem("s_ids")
        s_ids_f = sem("s_ids_f")
        s_spare = sem("s_spare")
        s_masked = sem("s_masked")
        s_w = sem("s_w")
        s_b2 = sem("s_b2")
        s_edges = [sem(f"s_edges{n}") for n in range(2)]
        s_hi = sem("s_hi")
        s_rest = sem("s_rest")
        s_mid = sem("s_mid")
        s_parts = sem("s_parts")
        s_cur = sem("s_cur")
        s_row = sem("s_row")
        s_row_act = sem("s_row_act")
        s_same = sem("s_same")
        s_distance = sem("s_distance")
        s_same_before = sem("s_same_before")
        s_count = sem("s_count")
        s_off = sem("s_off")
        s_target = sem("s_target")
        s_early_target = sem("s_early_target")
        s_summed = sem("s_summed")
        s_sums = sem("s_sums")
        s_early_sums = sem("s_early_sums")
        s_added = sem("s_added")
        s_issuing = sem("s_issuing")
        s_adding = sem("s_adding")
        s_landed = sem("s_landed")
        s_kept = sem("s_kept")
        s_kept_offset = sem("s_kept_offset")
        s_bounds = sem("s_bounds")
        s_broken = sem("s_broken")
        s_broken_all = sem("s_broken_all")
        s_rising = sem("s_rising")
        s_start = sem("s_start")
        s_e_offset = sem("s_e_offset")
        s_e_sums = sem("s_e_sums")
        s_e_added = sem("s_e_added")
        s_e_landed = sem("s_e_landed")
        s_x = [sem(f"s_x{n}") for n in range(SLOTS)]
        s_agg = [sem(f"s_agg{n}") for n in range(SLOTS)]
        s_stored = [sem(f"s_stored{n}") for n in range(SLOTS)]
        s_total = sem("s_total")
        s_mean = sem("s_mean")
        s_xc = sem("s_xc")
        s_sq = sem("s_sq")
        s_relu = sem("s_relu")
        s_var = sem("s_var")
        s_std = sem("s_std")
        s_ssq = sem("s_ssq")
        s_newton = sem("s_newton")
        s_xb = sem("s_xb")
        s_rstd = sem("s_rstd")
        s_h = sem("s_h")
        s_tr = sem("s_tr")
        s_feat = sem("s_feat")
        s_mm1 = sem("s_mm1")
        s_hid = sem("s_hid")
        s_mm2 = sem("s_mm2")
        s_y = sem("s_y")

        block = ctx.enter_context(nc.Block())

        def row_bank(l):
            return banks[:, 2 * l:2 * l + 2, :].rearrange("p b n -> p (b n)")

        row_bank_act = banks[:, 4:6, :].rearrange("p b n -> p (b n)")

        def sum_bank(l):
            return banks[:, 6 + l, 0:EC * D]

        def at_least(eng, semaphore, value):
            if not isinstance(value, int) or value > 0:
                eng.wait_ge(semaphore, value)

        def edge_steps(eng, body, steps=2, tail=0):
            rounds = N_BATCH // steps - tail
            for h in range(steps):
                body(0, h)
            with eng.Fori(1, rounds) as i:
                for h in range(steps):
                    body(i, h)
            for j in range(steps * rounds, N_BATCH):
                body(j // steps, j % steps)

        def is_batch(j):
            return not isinstance(j, int) or j < N_BATCH

        rounds = (N_TILES - 1) // SLOTS
        late_tail = rounds - (N_BATCH - EARLY) // 2

        def tile_steps(eng, body, tail=late_tail):
            for tt in range(SLOTS):
                body(0, tt)
            with eng.Fori(1, rounds - tail) as i:
                for tt in range(SLOTS):
                    body(i, tt)
            for i in range(rounds - tail, rounds):
                for tt in range(SLOTS):
                    body(i, tt)
            body(rounds, 0)

        def exists(tile):
            return not isinstance(tile, int) or 0 <= tile < N_TILES

        def first_node(tile):
            return max(0, N_NODES - TILE * (tile + 1)) if isinstance(tile, int) else N_NODES - TILE - tile * TILE

        def late_add(i, tt):
            n = N_BATCH + EARLY + 2 * i + tt // 2
            return None if tt % 2 or (isinstance(n, int) and n >= 2 * N_BATCH) else n

        @block.sync
        def _(sp):
            ids = [src, dst]
            for l in range(2):
                sp.dma_start(nodes_i[:, l, 1:N_BATCH, :],
                             ids[l][NEW:N_EDGES].rearrange("(b p c) -> p b c", p=P, c=EC)).then_inc(s_ids, 16)
                sp.dma_start(nodes_i[:, l, 0, :].rearrange("p (k c) -> p k c", k=2),
                             ids[l][0:BATCH].rearrange("(k p c) -> p k c", k=2, c=LAST_EC)).then_inc(s_ids, 16)

            def load_edges(h, j):
                if isinstance(j, int) and j == N_BATCH - 1:
                    sp.dma_start(edges[:, h, :, :].rearrange("p (k c) f -> p k c f", k=2),
                                 edge_attr[0:BATCH, :].rearrange("(k p c) f -> p k c f", k=2, c=LAST_EC))\
                        .then_inc(s_edges[h], 16)
                    return
                first = N_EDGES - BATCH - j * BATCH
                sp.dma_start(edges[:, h, :, :],
                             edge_attr[bass.ds(first, BATCH), :].rearrange("(p c) f -> p c f", c=EC))\
                    .then_inc(s_edges[h], 16)

            load_edges(0, 0)
            load_edges(1, 1)
            def load_x(i, tt):
                tile = SLOTS * i + tt
                if not exists(tile):
                    return
                at_least(sp, s_xc, tile - (SLOTS - 1))
                at_least(sp, s_xb, tile - (SLOTS - 1))
                sp.sem_inc(s_issuing, 1)
                sp.dma_start(xt[:, tt % SLOTS, :, :],
                             x[bass.ds(first_node(tile), TILE), :].rearrange("(p r) f -> p r f", r=R))\
                    .then_inc(s_x[tt % SLOTS], 16)

            sp.wait_ge(s_zero_src, 1)
            agg_flat = agg.rearrange("a f -> (a f)")

            def fill(first, last):
                for k in range(first, last):
                    n = P * ZERO_COLS
                    start = n * (ZERO_PARTS - 1 - k)
                    at_least(sp, s_zeroed[k % 2], 16 * (k // 2))
                    sp.dma_start(agg_flat[start:start + n].rearrange("(p f) -> p f", p=P), zeros)\
                        .then_inc(s_zeroed[k % 2], 16)

            fill(0, ZERO_FIRST)
            sp.dma_start(b2_all[:, :], b2.rearrange("(a n) -> a n", a=1).to_broadcast([P, D])).then_inc(s_b2, 16)
            sp.dma_start(w1_sb[:, :], w1[:, :]).then_inc(s_w, 16)
            sp.dma_start(w2_sb[:, :], w2[:, :]).then_inc(s_w, 16)
            sp.dma_start(b1_sb[:, :], b1.rearrange("(p a) -> p a", a=1)).then_inc(s_w, 16)

            def step(i, h):
                if is_batch(RING * i + (h + 2)):
                    sp.wait_ge(s_parts, RING * i + (h + 1))
                    load_edges(h % 2, RING * i + (h + 2))
                if isinstance(i, int) and i == 0:
                    first = ZERO_FIRST + ZERO_STEP * h
                    fill(first, min(first + ZERO_STEP, ZERO_PARTS))
                if isinstance(i, int) and i == N_BATCH // RING - 1 and h < SLOTS:
                    load_x(0, h)
            edge_steps(sp, step, RING, tail=1)

            def load_agg(i, tt):
                tile = SLOTS * i + tt
                if not exists(tile):
                    return
                at_least(sp, s_tr, GROUPS * tile - GROUPS * (SLOTS - 1))
                sp.sem_inc(s_issuing, 1)
                if isinstance(tile, int):
                    sp.wait_ge(s_landed, N_BATCH + min(N_BATCH, max(EARLY, dst_adds_before(tile))))
                else:
                    sp.wait_ge(s_landed, N_BATCH + EARLY - 1 + tt // 2 + 2 * i)
                sp.sem_inc(s_issuing, 1)
                sp.dma_start(ha[:, tt % SLOTS, :, 1, :],
                             agg[bass.ds(first_node(tile), TILE), :].rearrange("(p r) f -> p r f", r=R))\
                    .then_inc(s_agg[tt % SLOTS], 16)

            load_x(0, SLOTS)
            load_x(0, SLOTS + 1)
            sp.wait_ge(s_summed, 2 * N_BATCH)
            sp.wait_ge(s_start, 1)
            for tt in range(SLOTS - 1):
                load_agg(0, tt)

            def step(i, tt):
                t = SLOTS * i + tt
                s = tt % SLOTS
                load_agg(i, tt + SLOTS - 1)
                load_x(i, tt + SLOTS + 2)
                sp.wait_ge(s_y, GROUPS * t + GROUPS)
                sp.sem_inc(s_issuing, 1)
                if isinstance(t, int) and t == N_TILES - 1:
                    sp.wait_ge(s_stored[(s + SLOTS - 1) % SLOTS], 16 * (N_TILES // SLOTS))
                sp.dma_start(out[bass.ds(first_node(t), TILE), :].rearrange("(p r) f -> p r f", r=R), yt[:, s, :, :])\
                    .then_inc(s_stored[s], 16)
            tile_steps(sp, step, tail=2)
            for s in range(SLOTS):
                sp.wait_ge(s_stored[s], 16 * len(range(s, N_TILES, SLOTS)))

        @block.gpsimd
        def _(pool):
            pool.memset(ident[:, :], 0.0).then_inc(s_filled, 1)
            pool.memset(earlier[:, :], 1.0).then_inc(s_filled, 1)
            pool.wait_ge(s_filled, 2)
            pool.affine_select(out=ident[:, :], in_=ident[:, :], compare_op=ALU.not_equal, fill=1.0,
                               base=0, pattern=[[-1, P]], channel_multiplier=1).then_inc(s_const, 1)
            pool.affine_select(out=earlier[:, :], in_=earlier[:, :], compare_op=ALU.is_ge, fill=0.0,
                               base=BATCH - P, pattern=[[-1, BATCH]], channel_multiplier=1).then_inc(s_const, 1)
            pool.iota(spare_i[:, :], pattern=[[P, EC]], base=SPARE, channel_multiplier=1).then_inc(s_spare, 1)
            later = N_BATCH - EARLY
            pool.iota(bounds_i[:, 0:later, :], pattern=[[2 * TILE, later], [0, EC]],
                      base=bound(N_BATCH - 1), channel_multiplier=0).then_inc(s_bounds, 1)
            pool.iota(bounds_i[:, later:N_BATCH, :], pattern=[[low_bound(0) - low_bound(1), EARLY], [0, EC]],
                      base=low_bound(EARLY - 1), channel_multiplier=0).then_inc(s_bounds, 1)
            pool.memset(ones[:, :], 1.0).then_inc(s_ones, 1)
            pool.wait_ge(s_broken, 1)
            last = nodes_f[:, :, 0, 0:LAST_EC]
            pool.affine_select(out=last, in_=last, compare_op=ALU.is_ge, fill=float(PARK), base=NEW - 1,
                               pattern=[[0, 2], [-1, LAST_EC]], channel_multiplier=-LAST_EC).then_inc(s_masked, 1)
            pool.memset(nodes_f[:, :, 0, LAST_EC:EC], float(PARK)).then_inc(s_masked, 1)

            def spread(a):
                return a.unsqueeze(2).to_broadcast([P, R, D])

            def scale(i, tt):
                tile = SLOTS * i + tt
                if not exists(tile):
                    return
                s = tt % SLOTS
                pool.wait_ge(s_relu, tile + 1)
                pool.wait_ge(s_rstd, tile + 1)
                at_least(pool, s_tr, GROUPS * tile - GROUPS * (SLOTS - 1))
                pool.tensor_tensor(out=ha[:, s, :, 0, :], in0=xc[:, s, :, :], in1=spread(stat[:, s, 7, :]),
                                   op=ALU.mult).then_inc(s_h, 1)

            last_by_src = EARLY + N_BATCH - 1
            last_by_dst = 2 * N_BATCH - 1

            def chunks(n):
                last = isinstance(n, int) and n in (last_by_src, last_by_dst)
                return LAST_EC if last else EC

            def start_add(n, slot):
                if isinstance(n, int) and n < EARLY:
                    pool.wait_ge(s_early_target, n + 1)
                    pool.wait_ge(s_early_sums, n + 1)
                else:
                    pool.wait_ge(s_target, n + (1 - EARLY))
                    pool.wait_ge(s_sums, n + (1 - EARLY))
                pool.sem_inc(s_adding, 1)
                for c in range(chunks(n)):
                    pool.indirect_dma_start(
                        agg[:, :], bass.IndirectOffsetOnAxis(ap=target[:, slot, c:c + 1], axis=0),
                        sums[:, slot, c, :], None, compute_op=ALU.add).then_inc(s_added, 16)

            def end_add(n, late=True):
                missing = 16 * (EC - LAST_EC)
                if (not late) and not (isinstance(n, int) and n == last_by_src):
                    missing = 0
                if isinstance(n, int) and n == last_by_dst:
                    missing *= 2
                pool.wait_ge(s_added, 16 * EC * n + (16 * EC - missing))
                pool.sem_inc(s_landed, 1)

            def add_step(i, h):
                n = RING * i + (h + EARLY)
                start_add(n, (h + EARLY) % RING)
                end_add(n, late=False)

            def step(i, tt):
                scale(i, tt + AHEAD - 2)
                if late_add(i, tt) is not None:
                    start_add(late_add(i, tt), tt // 2)
                elif late_add(i, tt - 1) is not None:
                    end_add(late_add(i, tt - 1))

            def wait_zeros(fills):
                for n in range(2):
                    pool.wait_ge(s_zeroed[n], 16 * len(range(n, fills, 2)))

            for n in range(EARLY):
                wait_zeros(fills_before(n))
                start_add(n, n)
                end_add(n, late=False)
            wait_zeros(ZERO_PARTS)
            edge_steps(pool, add_step, RING)
            pool.wait_ge(s_summed, 2 * N_BATCH)
            scale(0, 0)
            scale(0, 1)
            pool.wait_ge(s_rising, 2)
            with pool.If(pool.value_load(falls[0:1, 0:1], min_val=0, max_val=2 * N_EDGES) > 0):
                pool.sem_inc(s_e_landed, 1)
                with pool.Fori(0, N_BATCH) as k:
                    pool.wait_ge(s_e_offset, k + 1)
                    pool.wait_ge(s_e_sums, k + 1)
                    pool.sem_inc(s_adding, 1)
                    for c in range(EC):
                        pool.indirect_dma_start(
                            agg[:, :], bass.IndirectOffsetOnAxis(ap=target[:, 0, c:c + 1], axis=0),
                            sums[:, 0, c, :], None, compute_op=ALU.add).then_inc(s_e_added, 16)
                    pool.wait_ge(s_e_added, 16 * EC * k + 16 * EC)
                    pool.sem_inc(s_e_landed, 1)
            pool.sem_inc(s_start, 1)
            tile_steps(pool, step)

        @block.vector
        def _(dve):
            nc.vector.memset(zeros, 0.0).then_inc(s_zero_src, 1)
            dve.wait_ge(s_ids, 64)
            nc.vector.tensor_copy(nodes_f[:, :, :, :], nodes_i[:, :, :, :]).then_inc(s_ids_f, 1)
            dve.wait_ge(s_spare, 1)
            nc.vector.tensor_copy(spare[:, :], spare_i[:, :]).then_inc(s_spare, 1)
            dve.wait_ge(s_bounds, 2)
            nc.vector.tensor_copy(bounds[:, :, :], bounds_i[:, :, :]).then_inc(s_bounds, 1)
            dve.wait_ge(s_bounds, 3)
            dve.wait_ge(s_ids_f, 1)
            later = N_BATCH - EARLY
            nc.vector.tensor_tensor(out=broken[:, 0:later, :], in0=nodes_f[:, 1, 0:later, :],
                                    in1=bounds[:, 0:later, :], op=ALU.is_ge).then_inc(s_broken, 1)
            nc.vector.tensor_tensor(out=broken[:, later:N_BATCH, :], in0=nodes_f[:, 1, later:N_BATCH, :],
                                    in1=bounds[:, later:N_BATCH, :], op=ALU.is_lt).then_inc(s_broken, 1)
            dve.wait_ge(s_broken, 2)
            nc.vector.tensor_reduce(out=broken_sum[:, :], in_=broken[:, :, :].rearrange("p b c -> p (b c)"),
                                    axis=AX.X, op=ALU.add).then_inc(s_broken, 1)
            dve.wait_ge(s_broken_all, 1)
            nc.vector.tensor_copy(falls[:, :], banks[:, 7, 0:1]).then_inc(s_rising, 1)
            nc.vector.tensor_scalar(rising[:, :], banks[:, 7, 0:1], 0.0, None, ALU.is_equal).then_inc(s_rising, 1)

            def split_mid(b, h):
                dve.wait_ge(s_hi, b + 1)
                nc.vector.tensor_tensor(out=rest[:, :, :], in0=edges[:, h, :, :], in1=parts[:, h, 0, :, :],
                                        op=ALU.subtract).then_inc(s_rest, 1)

            def split_lo(b, h):
                dve.wait_ge(s_mid, b + 1)
                nc.vector.tensor_tensor(out=parts[:, h, 2, :, :], in0=rest[:, :, :], in1=parts[:, h, 1, :, :],
                                        op=ALU.subtract).then_inc(s_parts, 1)

            def with_b2(i, tt):
                tile = SLOTS * i + tt
                if not exists(tile):
                    return
                s = tt % SLOTS
                at_least(dve, s_y, GROUPS * tile - GROUPS * (SLOTS - 1))
                nc.vector.tensor_tensor(out=xb[:, s, :, :], in0=xt[:, s, :, :],
                                        in1=b2_all[:, :].unsqueeze(1).to_broadcast([P, R, D]), op=ALU.add)\
                    .then_inc(s_xb, 1)

            def mean(i, tt):
                tile = SLOTS * i + tt
                if not exists(tile):
                    return
                s = tt % SLOTS
                dve.wait_ge(s_x[s], 16 * i + 16 * (1 + tt // SLOTS))
                nc.vector.tensor_reduce(out=stat[:, s, 0, :], in_=xt[:, s, :, :], axis=AX.X, op=ALU.add)\
                    .then_inc(s_total, 1)
                dve.wait_ge(s_total, tile + 1)
                nc.vector.tensor_scalar(stat[:, s, 1, :], stat[:, s, 0, :], -1.0 / D, None, ALU.mult)\
                    .then_inc(s_mean, 1)

            def center(i, tt):
                tile = SLOTS * i + tt
                if not exists(tile):
                    return
                s = tt % SLOTS
                dve.wait_ge(s_mean, tile + 1)
                at_least(dve, s_h, tile - (SLOTS - 1))
                nc.vector.tensor_tensor(out=xc[:, s, :, :], in0=xt[:, s, :, :],
                                        in1=stat[:, s, 1, :].unsqueeze(2).to_broadcast([P, R, D]),
                                        op=ALU.add).then_inc(s_xc, 1)

            def variance(i, tt):
                tile = SLOTS * i + tt
                if not exists(tile):
                    return
                s = tt % SLOTS
                dve.wait_ge(s_sq, tile + 1)
                nc.vector.tensor_reduce(out=stat[:, s, 2, :], in_=sq[:, tt % 2, :, :], axis=AX.X, op=ALU.add)\
                    .then_inc(s_ssq, 1)
                dve.wait_ge(s_ssq, tile + 1)
                nc.vector.tensor_scalar(stat[:, s, 3, :], stat[:, s, 2, :], 1.0 / D, EPS, ALU.mult, ALU.add)\
                    .then_inc(s_var, 1)

            def inverse(i, tt):
                tile = SLOTS * i + tt
                if not exists(tile):
                    return
                st = stat[:, tt % SLOTS, :, :]
                dve.wait_ge(s_std, tile + 1)
                nc.vector.reciprocal(st[:, 5, :], st[:, 4, :]).then_inc(s_newton, 1)
                dve.wait_ge(s_newton, 4 * tile + 1)
                nc.vector.tensor_tensor(out=st[:, 6, :], in0=st[:, 5, :], in1=st[:, 5, :], op=ALU.mult)\
                    .then_inc(s_newton, 1)
                dve.wait_ge(s_newton, 4 * tile + 2)
                nc.vector.tensor_tensor(out=st[:, 6, :], in0=st[:, 6, :], in1=st[:, 3, :], op=ALU.mult)\
                    .then_inc(s_newton, 1)
                dve.wait_ge(s_newton, 4 * tile + 3)
                nc.vector.tensor_scalar(st[:, 6, :], st[:, 6, :], -0.5, 1.5, ALU.mult, ALU.add).then_inc(s_newton, 1)
                dve.wait_ge(s_newton, 4 * tile + 4)
                at_least(dve, s_h, tile - (SLOTS - 1))
                nc.vector.tensor_tensor(out=st[:, 7, :], in0=st[:, 6, :], in1=st[:, 5, :], op=ALU.mult)\
                    .then_inc(s_rstd, 1)

            def prepare(tt):
                mean(0, tt + AHEAD)
                inverse(0, tt + AHEAD - 2)
                center(0, tt + AHEAD)
                with_b2(0, tt + AHEAD - 1)
                variance(0, tt + AHEAD - 1)

            split_mid(0, 0)
            split_lo(0, 0)
            dve.wait_ge(s_const, 2)
            dve.wait_ge(s_spare, 2)

            def set_target(n, slot, offsets, scalar, slots, ready):
                at_least(dve, s_landed, n + (1 - slots))
                nc.vector.scalar_tensor_tensor(out=target[:, slot, :], in0=offsets, scalar=scalar,
                                               in1=spare[:, :], op0=ALU.mult, op1=ALU.add).then_inc(ready, 1)

            def kept_offsets(j):
                return kept_offset[:, j, :] if isinstance(j, int)\
                    else kept_offset[:, bass.ds(j, 1), :].rearrange("p a c -> p (a c)")

            def step(i, h):
                j = RING * i + h
                for l in range(2):
                    m = 2 * j + l
                    dve.wait_ge(s_row, m + 1)
                    at_least(dve, s_summed, m - 1)
                    for c in range(EC):
                        first = P * c if c >= ACT_FROM else 0
                        last = P * (c + 1)
                        nc.vector.scalar_tensor_tensor(
                            out=same[:, l, c, first:last], in0=row_bank(l)[:, first:last],
                            scalar=cur[:, l, c:c + 1], in1=earlier[:, BATCH - last + first:BATCH],
                            op0=ALU.is_equal, op1=ALU.mult, accum_out=count[:, l, c:c + 1]).then_inc(s_same, 1)
                    at_least(dve, s_kept_offset, m)
                    nc.vector.tensor_tensor(out=offset[:, :], in0=cur[:, l, :], in1=spare[:, :],
                                            op=ALU.subtract).then_inc(s_off, 1)
                    dve.wait_ge(s_off, m + 1)
                    dve.wait_ge(s_same, EC * m + EC)
                    dve.wait_ge(s_same_before, (EC - ACT_FROM) * m + (EC - ACT_FROM))
                    nc.vector.tensor_tensor(out=count[:, l, ACT_FROM:EC], in0=count[:, l, ACT_FROM:EC],
                                            in1=count_before[:, l, :], op=ALU.add).then_inc(s_count, 1)
                    dve.wait_ge(s_count, m + 1)
                    if l == 0:
                        kept = src_offset[:, h % 2, :]
                        at_least(dve, s_target, j - 1)
                    else:
                        kept = kept_offsets(j)
                    nc.vector.scalar_tensor_tensor(out=kept, in0=count[:, l, :], scalar=1.0, in1=offset[:, :],
                                                   op0=ALU.is_equal, op1=ALU.mult).then_inc(s_kept_offset, 1)
                    if l == 0:
                        dve.wait_ge(s_kept_offset, m + 1)
                        set_target(j + EARLY, (h + EARLY) % RING, src_offset[:, h % 2, :], 1.0, RING, s_target)
                    elif isinstance(j, int) and j < EARLY:
                        dve.wait_ge(s_kept_offset, m + 1)
                        set_target(j, j, kept, rising[:, 0:1], RING, s_early_target)
                    if is_batch(j + 1):
                        if l == 0:
                            split_mid(j + 1, 1 - h % 2)
                        else:
                            split_lo(j + 1, 1 - h % 2)
            edge_steps(dve, step, RING)
            dve.wait_ge(s_b2, 16)
            for tt in range(-AHEAD, 0):
                prepare(tt)
            with dve.If(dve.value_load(falls[0:1, 0:1], min_val=0, max_val=2 * N_EDGES) > 0):
                dve.wait_ge(s_landed, N_BATCH + EARLY)
                with dve.Fori(0, N_BATCH) as k:
                    dve.wait_ge(s_e_landed, k + 1)
                    nc.vector.scalar_tensor_tensor(out=target[:, 0, :], in0=kept_offsets(k), scalar=1.0,
                                                   in1=spare[:, :], op0=ALU.mult, op1=ALU.add).then_inc(s_e_offset, 1)
                dve.wait_ge(s_e_landed, N_BATCH + 1)

            def finish(i, tt, g):
                t = SLOTS * i + tt
                s = tt % SLOTS
                k = GROUPS * t + g
                dve.wait_ge(s_mm2, k + 1)
                if g == 0:
                    at_least(dve, s_stored[s], 16 * i + 16 * (tt // SLOTS))
                rows = slice(GR * g, GR * g + GR)
                nc.vector.tensor_tensor(out=yt[:, s, rows, :],
                                        in0=banks[:, 4 + g % 2, 0:GR * D].rearrange("p (r f) -> p r f", f=D),
                                        in1=xb[:, s, rows, :], op=ALU.add).then_inc(s_y, 1)

            def step(i, tt):
                t = SLOTS * i + tt
                n = late_add(i, tt)
                if n is not None:
                    set_target(n, tt // 2, kept_offsets(n - N_BATCH), rising[:, 0:1], 2, s_target)
                for g in range(GROUPS):
                    if g == 0:
                        mean(i, tt + AHEAD)
                    if g == 1:
                        inverse(i, tt + AHEAD - 2)
                        center(i, tt + AHEAD)
                    if g == 2:
                        with_b2(i, tt + AHEAD - 1)
                    if g == 3:
                        variance(i, tt + AHEAD - 1)
                    finish(i, tt, g)
            tile_steps(dve, step)

        @block.scalar
        def _(act):
            def current(m, l, j):
                at_least(act, s_off, m - 1)
                b = N_BATCH - 1 - j
                nc.scalar.copy(cur[:, l, :], nodes_f[:, l, b, :] if isinstance(b, int)
                               else nodes_f[:, l, bass.ds(b, 1), :].rearrange("p a c -> p (a c)")).then_inc(s_cur, 1)

            def compare(m, l):
                act.wait_ge(s_row_act, m + 1)
                at_least(act, s_summed, m - 1)
                at_least(act, s_count, m - 1)
                first = (EC - ACT_FROM) * m
                for c in range(ACT_FROM, EC):
                    nc.scalar.activation(distance[c - ACT_FROM][:, 0:P * c], row_bank_act[:, 0:P * c], ACT.Square,
                                         bias=cur[:, l, c:c + 1], scale=-1.0).then_inc(s_distance, 1)
                for c in range(ACT_FROM, EC):
                    n = c - ACT_FROM
                    act.wait_ge(s_distance, first + n + 1)
                    nc.scalar.activation(same[:, l, c, 0:P * c], distance[n][:, 0:P * c], ACT.Relu,
                                         bias=ones[:, 0:1], scale=-2.0, accum_out=count_before[:, l, n:n + 1])\
                        .then_inc(s_same_before, 1)

            def split(i, h):
                j = RING * i + h
                s = h % 2
                act.wait_ge(s_edges[s], 16 * (RING // 2) * i + 16 * (1 + h // 2))
                at_least(act, s_summed, 2 * j - 2)
                nc.scalar.copy(parts[:, s, 0, :, :], edges[:, s, :, :]).then_inc(s_hi, 1)
                act.wait_ge(s_rest, j + 1)
                nc.scalar.copy(parts[:, s, 1, :, :], rest[:, :, :]).then_inc(s_mid, 1)

            def kept(j):
                k = kept_sums[:, j, :, :] if isinstance(j, int)\
                    else kept_sums[:, bass.ds(j, 1), :, :].rearrange("p a c f -> p (a c) f")
                return k.rearrange("p c f -> p (c f)")

            def set_sums(n, slot, source, slots, ready):
                at_least(act, s_landed, n + (1 - slots))
                nc.scalar.copy(sums[:, slot, :, :].rearrange("p c f -> p (c f)"), source).then_inc(ready, 1)

            def square(i, tt):
                tile = SLOTS * i + tt
                if not exists(tile):
                    return
                act.wait_ge(s_xc, tile + 1)
                at_least(act, s_ssq, tile - 1)
                nc.scalar.activation(sq[:, tt % 2, :, :], xc[:, tt % SLOTS, :, :], ACT.Square).then_inc(s_sq, 1)

            def relu(i, tt):
                tile = SLOTS * i + tt
                if not exists(tile):
                    return
                s = tt % SLOTS
                act.wait_ge(s_sq, tile + 1)
                nc.scalar.activation(xc[:, s, :, :], xc[:, s, :, :], ACT.Relu).then_inc(s_relu, 1)

            def root(i, tt):
                tile = SLOTS * i + tt
                if not exists(tile):
                    return
                s = tt % SLOTS
                act.wait_ge(s_var, tile + 1)
                nc.scalar.activation(stat[:, s, 4, :], stat[:, s, 3, :], ACT.Sqrt).then_inc(s_std, 1)

            def prepare(tt):
                relu(0, tt + AHEAD - 1)
                root(0, tt + AHEAD - 2)
                square(0, tt + AHEAD)

            act.wait_ge(s_masked, 2)
            current(0, 0, 0)
            current(1, 1, 0)
            split(0, 0)
            act.wait_ge(s_ones, 1)
            compare(0, 0)

            def step(i, h):
                j = RING * i + h
                for l in range(2):
                    m = 2 * j + l
                    if is_batch(j + 1):
                        current(m + 2, l, j + 1)
                        if l == 0:
                            split(i, h + 1)
                    if l == 0 or is_batch(j + 1):
                        compare(m + 1, 1 - l)
                    act.wait_ge(s_summed, m + 1)
                    if l == 0:
                        set_sums(j + EARLY, (h + EARLY) % RING, sum_bank(l), RING, s_sums)
                    else:
                        nc.scalar.copy(kept(j), sum_bank(l)).then_inc(s_kept, 1)
                        if isinstance(j, int) and j < EARLY:
                            act.wait_ge(s_kept, j + 1)
                            set_sums(j, j, kept(j), RING, s_early_sums)
            edge_steps(act, step, RING)
            act.wait_ge(s_kept, N_BATCH)
            for tt in range(-AHEAD, 0):
                prepare(tt)
            act.wait_ge(s_rising, 2)
            with act.If(act.value_load(falls[0:1, 0:1], min_val=0, max_val=2 * N_EDGES) > 0):
                act.wait_ge(s_landed, N_BATCH + EARLY)
                with act.Fori(0, N_BATCH) as k:
                    act.wait_ge(s_e_landed, k + 1)
                    nc.scalar.copy(sums[:, 0, :, :].rearrange("p c f -> p (c f)"), kept(k)).then_inc(s_e_sums, 1)
                act.wait_ge(s_e_landed, N_BATCH + 1)

            def feat(t, g):
                k = GROUPS * t + g
                act.wait_ge(s_tr, k + 1)
                at_least(act, s_mm1, k - 1)
                nc.scalar.copy(feat_T[:, g % 2, :], banks[:, g % 2, :]).then_inc(s_feat, 1)

            def hidden(t, g):
                k = GROUPS * t + g
                act.wait_ge(s_mm1, k + 1)
                if not (isinstance(k, int) and k < 2):
                    act.wait_ge(s_mm2, k - 1)
                nc.scalar.activation(hid_T[:, g % 2, :], banks[:, 2 + g % 2, :], ACT.Relu, bias=b1_sb[:, 0:1])\
                    .then_inc(s_hid, 1)

            act.wait_ge(s_w, 48)
            act.wait_ge(s_same_before, 2 * (EC - ACT_FROM) * N_BATCH)
            feat(0, 0)
            feat(0, 1)
            hidden(0, 0)

            def step(i, tt):
                t = SLOTS * i + tt
                for g in range(GROUPS):
                    if g < 2:
                        feat(t, g + 2)
                    elif exists(t + 1):
                        feat(t + 1, g - 2)
                    if g == 0:
                        if late_add(i, tt) is not None:
                            set_sums(late_add(i, tt), tt // 2, kept(late_add(i, tt) - N_BATCH), 2, s_sums)
                        relu(i, tt + AHEAD - 1)
                        root(i, tt + AHEAD - 2)
                    if g == 3:
                        square(i, tt + AHEAD)
                    if g < GROUPS - 1:
                        hidden(t, g + 1)
                    elif exists(t + 1):
                        hidden(t + 1, 0)
            tile_steps(act, step)

        @block.tensor
        def _(pe):
            def rows(m, l):
                pe.wait_ge(s_cur, m + 1)
                at_least(pe, s_same, EC * m - EC)
                for c in range(EC):
                    last = nc.tensor.transpose(row_bank(l)[:, P * c:P * (c + 1)],
                                               cur[:, l, c:c + 1].to_broadcast([P, P]), ident[:, :])
                last.then_inc(s_row, 1)
                at_least(pe, s_same_before, (EC - ACT_FROM) * m)
                for c in range(EC - 1):
                    last = nc.tensor.transpose(row_bank_act[:, P * c:P * (c + 1)],
                                               cur[:, l, c:c + 1].to_broadcast([P, P]), ident[:, :])
                last.then_inc(s_row_act, 1)

            pe.wait_ge(s_ones, 1)
            pe.wait_ge(s_broken, 3)
            nc.tensor.matmul(banks[:, 7, 0:1], ones[:, :], broken_sum[:, :], start=True, stop=True)\
                .then_inc(s_broken_all, 1)
            pe.wait_ge(s_const, 2)
            rows(0, 0)

            def step(i, h):
                j = 2 * i + h
                for l in range(2):
                    m = 2 * j + l
                    if l == 0 or is_batch(j + 1):
                        rows(m + 1, 1 - l)
                    pe.wait_ge(s_same, EC * m + EC)
                    pe.wait_ge(s_same_before, (EC - ACT_FROM) * m + (EC - ACT_FROM))
                    pe.wait_ge(s_parts, j + 1)
                    if l == 0:
                        at_least(pe, s_sums, j)
                    else:
                        at_least(pe, s_kept, j)
                    for c in range(EC):
                        for c2 in range(c, EC):
                            for k in range(3):
                                last = nc.tensor.matmul(sum_bank(l)[:, D * c:D * (c + 1)],
                                                        same[:, l, c2, P * c:P * (c + 1)], parts[:, h, k, c2, :],
                                                        start=(c2 == c and k == 0), stop=(c2 == EC - 1 and k == 2))
                    last.then_inc(s_summed, 1)
            edge_steps(pe, step)

            def transposes(i, tt, g):
                t = SLOTS * i + tt
                s = tt % SLOTS
                k = GROUPS * t + g
                if g == 0:
                    pe.wait_ge(s_h, t + 1)
                    pe.wait_ge(s_agg[s], 16 * i + 16 * (1 + tt // SLOTS))
                at_least(pe, s_feat, k - 1)
                for j in range(GR):
                    last = nc.tensor.transpose(banks[:, g % 2, P * j:P * (j + 1)],
                                               ha[:, s, GR * g + j, :, :].rearrange("p a f -> p (a f)"), ident[:, :])
                last.then_inc(s_tr, 1)

            def mm1(t, g):
                k = GROUPS * t + g
                pe.wait_ge(s_feat, k + 1)
                at_least(pe, s_hid, k - 1)
                nc.tensor.matmul(banks[:, 2 + g % 2, :], w1_sb[:, :], feat_T[:, g % 2, :],
                                 start=True, stop=True).then_inc(s_mm1, 1)

            def mm2(t, g):
                k = GROUPS * t + g
                pe.wait_ge(s_hid, k + 1)
                at_least(pe, s_y, k - 1)
                acc = banks[:, 4 + g % 2, 0:GR * D]
                for j in range(GR):
                    last = nc.tensor.matmul(acc[:, D * j:D * (j + 1)], hid_T[:, g % 2, P * j:P * (j + 1)],
                                            w2_sb[:, :], start=True, stop=True)
                last.then_inc(s_mm2, 1)

            pe.wait_ge(s_w, 48)
            transposes(0, 0, 0)
            transposes(0, 0, 1)
            mm1(0, 0)

            def step(i, tt):
                t = SLOTS * i + tt
                for g in range(GROUPS):
                    if g < 2:
                        transposes(i, tt, g + 2)
                    elif exists(t + 1):
                        transposes(i, tt + 1, g - 2)
                    if g < GROUPS - 1:
                        mm1(t, g + 1)
                    elif exists(t + 1):
                        mm1(t + 1, 0)
                    mm2(t, g)
            tile_steps(pe, step, tail=1)


_INS = ['x', 'src', 'dst', 'edge_attr_64', 'L0_gnn_W1', 'L0_gnn_b1', 'L0_gnn_W2', 'L0_gnn_b2']


def kernel(**inputs):
    import numpy as _np
    import concourse.bacc as _bacc
    from concourse import mybir as _mybir
    from concourse.bass_utils import run_bass_kernel_spmd as _run

    nc = _bacc.Bacc("TRN2", target_bir_lowering=False, num_devices=1)
    arrays, args = {}, []
    for name in _INS:
        a = _np.ascontiguousarray(inputs[name])
        arrays[f"in_{name}"] = a
        args.append(nc.dram_tensor(f"in_{name}", a.shape, _mybir.dt.from_np(a.dtype), kind="ExternalInput").ap())
    result = nc.dram_tensor("out", (N_NODES, D), _mybir.dt.float32, kind="ExternalOutput").ap()
    gnn_program(nc, *args, result)
    r = _run(nc, [arrays], core_ids=[0])
    return r.results[0]["out"]
```
